# Optimizing a Trainium2 kernel written in Bass

```python
import numpy as np
import jax
import jax.numpy as jnp

def _softmax(x, axis=-1):
    return jax.nn.softmax(x, axis=axis)

def _gelu(x):
    return jax.nn.gelu(x, approximate=True)

def _silu(x):
    return jax.nn.silu(x)

def _sigmoid(x):
    return jax.nn.sigmoid(x)

def _layernorm(x, axis=-1, eps=1e-05):
    m = jnp.mean(x, axis=axis, keepdims=True)
    v = jnp.var(x, axis=axis, keepdims=True)
    return (x - m) / jnp.sqrt(v + eps)

def _scatter_add(tgt, idx, src, axis=0):
    return tgt.at[idx].add(src)

def _segment_sum(src, seg, n):
    return jax.ops.segment_sum(src, seg, n)
kernel_name = 'mk_xattn_ffn_d1_seqx_r8_3313d6'

def setup_inputs(seed: int=0):
    np.random.seed(seed)
    _w = jnp.asarray

    def _rec_inputs():
        import jax
        import jax.numpy as jnp
        _rk = jax.random.key(seed)
        x = -0.0003929 + 0.9999 * jax.random.normal(jax.random.fold_in(_rk, 1), (4, 256, 128), jnp.float32)
        _lenS = 256 - jax.random.randint(jax.random.fold_in(_rk, 7), (4,), 0, max(1, 256 // 4) + 1, jnp.int32)
        _lenS2 = 256 - jax.random.randint(jax.random.fold_in(_rk, 8), (4,), 0, max(1, 256 // 4) + 1, jnp.int32)
        _ctx_1024P = jax.random.normal(jax.random.fold_in(_rk, 11), (4, 16, 128), jnp.float32)
        _ctx_1024c = jax.random.dirichlet(jax.random.fold_in(_rk, 511), 0.3 * jnp.ones((16,), jnp.float32), (4, 256))
        _ctx_1024t = jnp.einsum('bsk,bkd->bsd', _ctx_1024c, _ctx_1024P)
        _ctx_1024t = _ctx_1024t * jax.lax.rsqrt(jnp.mean(jnp.square(_ctx_1024t)) + 1e-12) * 0.953939
        ctx_1024 = 2.81802e-05 + 1.00001 * (_ctx_1024t + 0.3 * jax.random.normal(jax.random.fold_in(_rk, 611), (4, 256, 128), jnp.float32))
        return (x, ctx_1024)
    x, ctx_1024 = _rec_inputs()

    def _L0_xattn_setup():
        import jax, jax.numpy as jnp
        import numpy as np
        ATTN_WINDOW = 128
        HIDDEN = 128
        NUM_HEADS = 16

        def _sliding_window_attention(q, k, v, w):
            B, nh, S, D = q.shape
            nc = S // w
            k_pad = jnp.pad(k, ((0, 0), (0, 0), (w, w), (0, 0)))
            v_pad = jnp.pad(v, ((0, 0), (0, 0), (w, w), (0, 0)))
            idx = (jnp.arange(nc) * w)[:, None] + jnp.arange(3 * w)[None, :]
            k_c = k_pad[:, :, idx, :]
            v_c = v_pad[:, :, idx, :]
            q_c = q.reshape(B, nh, nc, w, D)
            scores = jnp.einsum('bhcid,bhcjd->bhcij', q_c, k_c)
            i = jnp.arange(w)[:, None]
            j = jnp.arange(3 * w)[None, :]
            band = jnp.abs(j - w - i) <= w
            key_pos = (jnp.arange(nc) * w)[:, None, None] + j[None, :, :] - w
            valid = band[None, :, :] & (key_pos >= 0) & (key_pos < S)
            big_neg = jnp.finfo(scores.dtype).min
            scores = jnp.where(valid[None, None], scores, big_neg)
            probs = jax.nn.softmax(scores, axis=-1)
            out = jnp.einsum('bhcij,bhcjd->bhcid', probs, v_c)
            return out.reshape(B, nh, S, D)
        key = jax.random.key(seed)
        k1, k2, k3 = jax.random.split(key, 3)
        B, S = (2, 1024)
        query = jax.random.normal(k1, (B, S, HIDDEN), dtype=jnp.float32)
        key_t = jax.random.normal(k2, (B, S, HIDDEN), dtype=jnp.float32)
        value = jax.random.normal(k3, (B, S, HIDDEN), dtype=jnp.float32)
        return {'query': query, 'key': key_t, 'value': value}
    _L0_xattn_all = _L0_xattn_setup()
    _L0_xattn_in = {k: v for k, v in _L0_xattn_all.items() if k in ()}
    del _L0_xattn_all

    def _L0_ffn_setup():
        import jax, jax.numpy as jnp
        import numpy as np
        D_MODEL = 128
        N_HEAD = 16
        HEAD_DIM = D_MODEL // N_HEAD
        D_FF = 512
        N_EXPERTS = 4
        EPS = 1e-05

        def _layer_norm(x, gamma, beta):
            mu = jnp.mean(x, axis=-1, keepdims=True)
            var = jnp.mean((x - mu) ** 2, axis=-1, keepdims=True)
            return (x - mu) / jnp.sqrt(var + EPS) * gamma + beta
        key = jax.random.key(seed)
        ks = jax.random.split(key, 20)
        f32 = jnp.float32
        sc = 1.0 / np.sqrt(D_MODEL)
        scf = 1.0 / np.sqrt(D_FF)
        return {'src': jax.random.normal(ks[0], (4, 64, D_MODEL), f32), 'Wq': jax.random.normal(ks[1], (D_MODEL, D_MODEL), f32) * sc, 'bq': jnp.zeros((D_MODEL,), f32), 'Wk': jax.random.normal(ks[2], (D_MODEL, D_MODEL), f32) * sc, 'bk': jnp.zeros((D_MODEL,), f32), 'Wv': jax.random.normal(ks[3], (D_MODEL, D_MODEL), f32) * sc, 'bv': jnp.zeros((D_MODEL,), f32), 'Wo': jax.random.normal(ks[4], (D_MODEL, D_MODEL), f32) * sc, 'bo': jnp.zeros((D_MODEL,), f32), 'router_w': jax.random.normal(ks[5], (D_MODEL, 1), f32) * 0.05, 'router_b': jnp.zeros((1,), f32), 'W1': jax.random.normal(ks[6], (N_EXPERTS, D_MODEL, D_FF), f32) * sc, 'b1': jnp.zeros((N_EXPERTS, D_FF), f32), 'W2': jax.random.normal(ks[7], (N_EXPERTS, D_FF, D_MODEL), f32) * scf, 'b2': jnp.zeros((N_EXPERTS, D_MODEL), f32), 'ln1_g': jnp.ones((D_MODEL,), f32), 'ln1_b': jnp.zeros((D_MODEL,), f32), 'ln2_g': jnp.ones((D_MODEL,), f32), 'ln2_b': jnp.zeros((D_MODEL,), f32)}
    _L0_ffn_all = _L0_ffn_setup()
    _L0_ffn_in = {k: v for k, v in _L0_ffn_all.items() if k in ('Wq', 'bq', 'Wk', 'bk', 'Wv', 'bv', 'Wo', 'bo', 'router_w', 'router_b', 'W1', 'b1', 'W2', 'b2', 'ln1_g', 'ln1_b', 'ln2_g', 'ln2_b')}
    del _L0_ffn_all
    return {'x': x, 'ctx_1024': ctx_1024, 'L0_ffn_Wq': _L0_ffn_in['Wq'], 'L0_ffn_bq': _L0_ffn_in['bq'], 'L0_ffn_Wk': _L0_ffn_in['Wk'], 'L0_ffn_bk': _L0_ffn_in['bk'], 'L0_ffn_Wv': _L0_ffn_in['Wv'], 'L0_ffn_bv': _L0_ffn_in['bv'], 'L0_ffn_Wo': _L0_ffn_in['Wo'], 'L0_ffn_bo': _L0_ffn_in['bo'], 'L0_ffn_router_w': _L0_ffn_in['router_w'], 'L0_ffn_router_b': _L0_ffn_in['router_b'], 'L0_ffn_W1': _L0_ffn_in['W1'], 'L0_ffn_b1': _L0_ffn_in['b1'], 'L0_ffn_W2': _L0_ffn_in['W2'], 'L0_ffn_b2': _L0_ffn_in['b2'], 'L0_ffn_ln1_g': _L0_ffn_in['ln1_g'], 'L0_ffn_ln1_b': _L0_ffn_in['ln1_b'], 'L0_ffn_ln2_g': _L0_ffn_in['ln2_g'], 'L0_ffn_ln2_b': _L0_ffn_in['ln2_b']}

def reference(x, ctx_1024, L0_ffn_Wq, L0_ffn_bq, L0_ffn_Wk, L0_ffn_bk, L0_ffn_Wv, L0_ffn_bv, L0_ffn_Wo, L0_ffn_bo, L0_ffn_router_w, L0_ffn_router_b, L0_ffn_W1, L0_ffn_b1, L0_ffn_W2, L0_ffn_b2, L0_ffn_ln1_g, L0_ffn_ln1_b, L0_ffn_ln2_g, L0_ffn_ln2_b):
    import jax
    import jax.numpy as jnp

    def _L0_xattn_ref(query, key, value):
        import jax, jax.numpy as jnp
        import numpy as np
        ATTN_WINDOW = 128
        HIDDEN = 128
        NUM_HEADS = 16

        def _sliding_window_attention(q, k, v, w):
            B, nh, S, D = q.shape
            nc = S // w
            k_pad = jnp.pad(k, ((0, 0), (0, 0), (w, w), (0, 0)))
            v_pad = jnp.pad(v, ((0, 0), (0, 0), (w, w), (0, 0)))
            idx = (jnp.arange(nc) * w)[:, None] + jnp.arange(3 * w)[None, :]
            k_c = k_pad[:, :, idx, :]
            v_c = v_pad[:, :, idx, :]
            q_c = q.reshape(B, nh, nc, w, D)
            scores = jnp.einsum('bhcid,bhcjd->bhcij', q_c, k_c)
            i = jnp.arange(w)[:, None]
            j = jnp.arange(3 * w)[None, :]
            band = jnp.abs(j - w - i) <= w
            key_pos = (jnp.arange(nc) * w)[:, None, None] + j[None, :, :] - w
            valid = band[None, :, :] & (key_pos >= 0) & (key_pos < S)
            big_neg = jnp.finfo(scores.dtype).min
            scores = jnp.where(valid[None, None], scores, big_neg)
            probs = jax.nn.softmax(scores, axis=-1)
            out = jnp.einsum('bhcij,bhcjd->bhcid', probs, v_c)
            return out.reshape(B, nh, S, D)
        B, S, _ = query.shape
        D = HIDDEN // NUM_HEADS
        q = query.reshape(B, S, NUM_HEADS, D).transpose(0, 2, 1, 3)
        k = key.reshape(B, S, NUM_HEADS, D).transpose(0, 2, 1, 3)
        v = value.reshape(B, S, NUM_HEADS, D).transpose(0, 2, 1, 3)
        out = _sliding_window_attention(q, k, v, ATTN_WINDOW)
        return out.transpose(0, 2, 1, 3).reshape(B, S, HIDDEN)

    def _L0_ffn_ref(src, Wq, bq, Wk, bk, Wv, bv, Wo, bo, router_w, router_b, W1, b1, W2, b2, ln1_g, ln1_b, ln2_g, ln2_b):
        import jax, jax.numpy as jnp
        import numpy as np
        D_MODEL = 128
        N_HEAD = 16
        HEAD_DIM = D_MODEL // N_HEAD
        D_FF = 512
        N_EXPERTS = 4
        EPS = 1e-05

        def _layer_norm(x, gamma, beta):
            mu = jnp.mean(x, axis=-1, keepdims=True)
            var = jnp.mean((x - mu) ** 2, axis=-1, keepdims=True)
            return (x - mu) / jnp.sqrt(var + EPS) * gamma + beta
        B, T, _ = src.shape
        q = (src @ Wq + bq).reshape(B, T, N_HEAD, HEAD_DIM)
        k = (src @ Wk + bk).reshape(B, T, N_HEAD, HEAD_DIM)
        v = (src @ Wv + bv).reshape(B, T, N_HEAD, HEAD_DIM)
        scale = HEAD_DIM ** (-0.5)
        scores = jnp.einsum('bqhd,bkhd->bhqk', q, k) * scale
        probs = jax.nn.softmax(scores, axis=-1)
        attn = jnp.einsum('bhqk,bkhd->bqhd', probs, v).reshape(B, T, D_MODEL)
        attn = attn @ Wo + bo
        x = _layer_norm(src + attn, ln1_g, ln1_b)
        keys = (x @ router_w + router_b)[..., 0]
        expert_idx = jnp.remainder(jnp.floor(keys).astype(jnp.int32), N_EXPERTS)
        ff_out = jnp.zeros_like(x)
        for e in range(N_EXPERTS):
            h = jax.nn.relu(x @ W1[e] + b1[e])
            y = h @ W2[e] + b2[e]
            ff_out = ff_out + jnp.where((expert_idx == e)[..., None], y, 0.0)
        return _layer_norm(x + ff_out, ln2_g, ln2_b)
    x = x + _L0_xattn_ref(_layernorm(x, axis=-1), ctx_1024, ctx_1024)
    x = x + _L0_ffn_ref(_layernorm(x, axis=-1), L0_ffn_Wq, L0_ffn_bq, L0_ffn_Wk, L0_ffn_bk, L0_ffn_Wv, L0_ffn_bv, L0_ffn_Wo, L0_ffn_bo, L0_ffn_router_w, L0_ffn_router_b, L0_ffn_W1, L0_ffn_b1, L0_ffn_W2, L0_ffn_b2, L0_ffn_ln1_g, L0_ffn_ln1_b, L0_ffn_ln2_g, L0_ffn_ln2_b)
    return x

_drawn_inputs = setup_inputs


def setup_inputs(seed=0):
    import zlib

    import numpy as np

    out = dict(_drawn_inputs(seed))
    spreads = {'L0_ffn_bq': (0.0, 0.314),
     'L0_ffn_bk': (0.0, 0.8),
     'L0_ffn_bv': (0.0, 0.1),
     'L0_ffn_bo': (0.0, 0.1),
     'L0_ffn_b1': (0.0, 0.378),
     'L0_ffn_b2': (0.0, 0.27),
     'L0_ffn_ln1_g': (1.0, 0.2),
     'L0_ffn_ln1_b': (0.0, 0.1),
     'L0_ffn_ln2_g': (1.0, 0.2),
     'L0_ffn_ln2_b': (0.0, 0.1)}
    factors = {}
    for name, (base, spread) in spreads.items():
        noise = np.random.default_rng([zlib.crc32(name.encode()), seed]).standard_normal(out[name].shape)
        drawn = base * np.exp(spread * noise) if base else spread * noise
        out[name] = jnp.asarray(drawn.astype(out[name].dtype))
    for name, factor in factors.items():
        out[name] = (out[name] * factor).astype(out[name].dtype)
    return out
```

```python
from contextlib import ExitStack

import numpy as np
import concourse.bass as bass
from concourse import mybir

ALU = mybir.AluOpType
ACT = mybir.ActivationFunctionType
AX = mybir.AxisListType
F32 = mybir.dt.float32
F32R = mybir.dt.float32r
BF16 = mybir.dt.bfloat16
I32 = mybir.dt.int32

P = 128
B, S = 4, 256
TT = S // P
D = 128
H = 16
HD = D // H
G = 4
HG = H // G
TERMS = 3
HR = TERMS * HD
GR = HG * HR
VC = 32
NE = 4
FF = 512
FC = FF // P
EPS = 1e-5
MASKED = -1.0e30
SCALE2 = float(HD) ** -0.5

ST_PER_BATCH = 40
SM_TAIL = 4
SM_PER_BATCH = 36 + SM_TAIL
MB_TAIL = 2
MB_PER_BATCH = 9 + MB_TAIL
MB_SETUP = 1


class Turn:

    def __init__(self, start):
        self.start, self.k = start, 0

    def next(self):
        n = self.start + self.k
        self.k += 1
        return n

    @property
    def slot(self):
        return self.k % 2


def sm_start(i):
    return 0 if isinstance(i, int) and i == 0 else i * SM_PER_BATCH - SM_TAIL


def mb_start(i):
    return 0 if isinstance(i, int) and i == 0 else i * MB_PER_BATCH + (MB_SETUP - MB_TAIL)


def passes(eng, body):
    body(0)
    for i in eng.Fori(1, B - 1):
        body(i)
    body(B - 1)
    body(B)


def unrolled(eng, body):
    for i in range(B + 1):
        body(i)


def is_first(i):
    return isinstance(i, int) and i == 0


def has_batch(i):
    return not (isinstance(i, int) and i == B)


def has_next(i):
    return not (isinstance(i, int) and i >= B - 1)


def build(nc, x, ctx_in, Wq, bq, Wk, bk, Wv, bv, Wo, bo, rw, rb, W1, b1, W2, b2, g1, be1, g2, be2, out,
          loop=unrolled):
    with ExitStack() as ctx:
        def sb(name, shape, dt=F32):
            return ctx.enter_context(nc.sbuf_tensor(name, shape, dt))

        def bank(name):
            return ctx.enter_context(nc.psum_tensor(name, [P, 512], F32))

        def sem(name):
            return ctx.enter_context(nc.semaphore(name))

        xb = sb("xb", [P, TT, D])
        cb = sb("cb", [P, TT, D])
        wqkv = sb("wqkv", [P, 3 * D])
        bqkv = sb("bqkv", [P, 3 * D])
        wo = sb("wo", [P, D])
        bo_b = sb("bo_b", [P, D])
        rw_b = sb("rw_b", [P, D])
        rb_b = sb("rb_b", [P, 1])
        g1_b = sb("g1_b", [P, D])
        be1_b = sb("be1_b", [P, D])
        g2_b = sb("g2_b", [P, D])
        be2_b = sb("be2_b", [P, D])
        w1 = sb("w1", [P, NE, FF])
        w2 = sb("w2", [P, NE, FC, D])
        b1_rows = sb("b1_rows", [NE * FC, P])
        b1_cols = sb("b1_cols", [P, NE * FC])
        b2_3 = sb("b2_3", [TERMS, NE * D])
        ident = sb("ident", [P, P])
        ident_b = sb("ident_b", [P, P], BF16)
        mask_above = sb("mask_above", [P, 2, P], BF16)
        mask_below = sb("mask_below", [P, 2, P], BF16)
        head_rows = sb("head_rows", [P, HG])
        half = sb("half", [P, TT])
        b2_part = sb("b2_part", [TERMS, 3, NE * D], BF16)
        b2_left = sb("b2_left", [TERMS, 2, NE * D])
        b2_sel = sb("b2_sel", [TERMS, 3])
        b2_pick = sb("b2_pick", [TERMS, 3, NE * D])
        b2_bf = sb("b2_bf", [TERMS, NE, D], BF16)
        ones_bf = sb("ones_bf", [TERMS, P], BF16)
        stats = [sb(f"stats{k}", [P, TT, 6]) for k in range(4)]
        mean_var = [sb(f"mean_var{k}", [P, TT, 2]) for k in range(4)]
        var_eps = [sb(f"var_eps{k}", [P, TT]) for k in range(4)]
        rstd = [sb(f"rstd{k}", [P, TT]) for k in range(4)]
        xn = sb("xn", [P, TT, D])
        q_tok = [sb(f"q_tok{a}", [P, TT, H * HR], F32R) for a in range(2)]
        k_tok = [sb(f"k_tok{a}", [P, TT, H * HR], F32R) for a in range(2)]
        q_rows = [sb(f"q_rows{a}", [P, G, S], F32R) for a in range(2)]
        k_rows = [sb(f"k_rows{a}", [GR, G, S]) for a in range(2)]
        keys_bd = [sb(f"keys_blockdiag{a}", [P, G, HG, S], F32R) for a in range(2)]
        values = [sb(f"values{a}", [P, TT, H, VC]) for a in range(2)]
        mx = sb("mx", [P, 2, TT, HG])
        mx_hi = sb("mx_hi", [P, 2, TT, P])
        probs = sb("probs", [P, 2, TT, HG, S])
        heads_t = sb("heads_t", [P, G, S])
        recip = sb("recip", [P, TT, H])
        att = sb("att", [P, TT, D])
        x1 = sb("x1", [P, B * TT * D])
        src = sb("src", [P, TT, D])
        src_bo = sb("src_bo", [P, TT, D])
        src_t = sb("src_t", [P, S])
        qkv = sb("qkv", [P, TT, 3 * D])
        att_t = sb("att_t", [P, S])
        res = sb("res", [P, TT, D])
        res_n = sb("res_n", [P, TT, D])
        h_scaled = sb("h_scaled", [P, TT, D])
        h = sb("h", [P, TT, D])
        h_t = sb("h_t", [P, S])
        junk = sb("junk", [P, TT, D])
        key = sb("key", [P, TT])
        key_b = sb("key_b", [P, TT])
        key_i = sb("key_i", [P, TT], I32)
        key_f = sb("key_f", [P, TT])
        key_gt = sb("key_gt", [P, TT])
        key_fl = sb("key_fl", [P, TT])
        key_fi = sb("key_fi", [P, TT], I32)
        expert = sb("expert", [P, TT], I32)
        expert_f = sb("expert_f", [P, TT])
        chosen = sb("chosen", [P, NE, TT])
        hid = sb("hid", [P, 2, 2, S])
        acc = sb("acc", [P, TT, D])
        acc_n = sb("acc_n", [P, TT, D])
        out_g = sb("out_g", [P, TT, D])
        out_b = sb("out_b", [P, TT, D])
        out_sb = sb("out_sb", [P, TT, D])
        ST = [bank(f"ST{k}") for k in range(2)]
        SM = [bank(f"SM{k}") for k in range(2)]
        PO = bank("PO")
        Y = bank("Y")
        UP = bank("UP")
        MB = bank("MB")
        x_in, c_in, w_in, wf_in = sem("x_in"), sem("c_in"), sem("w_in"), sem("wf_in")
        consts = sem("consts")
        consts_v = sem("consts_v")
        zeroed = sem("zeroed")
        sel_done = sem("sel_done")
        b2_step = sem("b2_step")
        st_full, st_done = sem("st_full"), sem("st_done")
        sm_full, sm_done = sem("sm_full"), sem("sm_done")
        mb_full, mb_done = sem("mb_full"), sem("mb_done")
        po_done = sem("po_done")
        up_full, up_done = sem("up_full"), sem("up_done")
        pv_done = sem("pv_done")
        down_done = sem("down_done")
        bn = [sem(f"bn{k}") for k in range(4)]
        ag = [sem(f"ag{k}") for k in range(4)]
        ve = [sem(f"ve{k}") for k in range(4)]
        rs = [sem(f"rs{k}") for k in range(4)]
        nm = [sem(f"nm{k}") for k in range(4)]
        hi_done = sem("hi_done")
        q_tok_done, k_tok_done = sem("q_tok_done"), sem("k_tok_done")
        v_done = sem("v_done")
        kbd_done = sem("kbd_done")
        mx_done = sem("mx_done")
        mxh_done = sem("mxh_done")
        mxl_done = sem("mxl_done")
        tri_done = sem("tri_done")
        recip_done, att_done = sem("recip_done"), sem("att_done")
        x1_done = sem("x1_done")
        srcbo_done = sem("srcbo_done")
        hs_done, h_done = sem("hs_done"), sem("h_done")
        route = sem("route")
        acc_done = sem("acc_done")
        og_done, ob_done = sem("og_done"), sem("ob_done")
        out_done, stored = sem("out_done"), sem("stored")

        block = ctx.enter_context(nc.Block())

        xr = x.rearrange("b (t p) d -> b p t d", p=P)
        cr = ctx_in.rearrange("b (t p) d -> b p t d", p=P)
        outr = out.rearrange("b (t p) d -> b p t d", p=P)
        W_ALL, WF_ALL = 16 * 14, 16 * 4
        CONST_V = 6 + 2 * G + 1
        ROUTE = TT + 8 + NE

        def x1_of(b):
            return x1[:, bass.ds(b * (TT * D), TT * D)].rearrange("p (t d) -> p t d", d=D)

        def row(v):
            return v.rearrange("(a d) -> a d", a=1).to_broadcast([P, D])

        @block.sync
        def _(sp):
            sp.dma_start(cb[:], cr[0]).then_inc(c_in, 16)
            sp.dma_start(xb[:], xr[0]).then_inc(x_in, 16)
            for k, w in enumerate((Wq, Wk, Wv)):
                sp.dma_start(wqkv[:, k * D:(k + 1) * D], w).then_inc(w_in, 16)
            for k, v in enumerate((bq, bk, bv)):
                sp.dma_start(bqkv[:, k * D:(k + 1) * D], row(v)).then_inc(w_in, 16)
            sp.dma_start(wo[:], Wo).then_inc(w_in, 16)
            for t, v in ((bo_b, bo), (g1_b, g1), (be1_b, be1), (g2_b, g2), (be2_b, be2)):
                sp.dma_start(t[:], row(v)).then_inc(w_in, 16)
            sp.dma_start(rw_b[:], row(rw.rearrange("d a -> (d a)"))).then_inc(w_in, 16)
            sp.dma_start(rb_b[:], rb.rearrange("(a d) -> a d", a=1).to_broadcast([P, 1])).then_inc(w_in, 16)
            sp.dma_start(b1_rows[:], b1.rearrange("e (c p) -> (e c) p", p=P)).then_inc(wf_in, 16)
            sp.dma_start(b2_3[:], b2.rearrange("e d -> (e d)").rearrange("(a n) -> a n", a=1)
                         .to_broadcast([TERMS, NE * D])).then_inc(wf_in, 16)
            sp.dma_start(w1[:], W1.rearrange("e d f -> d e f")).then_inc(wf_in, 16)
            sp.dma_start(w2[:], W2.rearrange("e (c p) d -> p e c d", p=P)).then_inc(wf_in, 16)

            def body(i):
                if has_next(i):
                    sp.wait_ge(k_tok_done, 2 * i + 1)
                    sp.wait_ge(v_done, 2 * i + 1)
                    sp.dma_start(cb[:], cr[i + 1]).then_inc(c_in, 16)
                    sp.wait_ge(x1_done, i + 1)
                    sp.dma_start(xb[:], xr[i + 1]).then_inc(x_in, 16)
                if not is_first(i):
                    sp.wait_ge(out_done, i)
                    sp.dma_start(outr[i - 1], out_sb[:]).then_inc(stored, 16)
            loop(sp, body)
            sp.wait_ge(stored, 16 * B)

        @block.gpsimd
        def _(pool):
            pool.memset(ident[:], 0.0).then_inc(zeroed, 1)
            pool.memset(head_rows[:], 1.0).then_inc(zeroed, 1)
            pool.wait_ge(zeroed, 2)
            pool.affine_select(out=ident[:], in_=ident[:], compare_op=ALU.not_equal, fill=1.0, base=0,
                               pattern=[[-1, P]], channel_multiplier=1).then_inc(consts, 1)
            pool.wait_ge(consts, 1)
            edges = ((0, GR, HR), (GR, P, 2))
            for k, (lo, hi, n) in enumerate(edges):
                rows = head_rows[lo:hi, :]
                pool.affine_select(out=rows, in_=rows, compare_op=ALU.is_ge, fill=0.0, base=0,
                                   pattern=[[-n, HG]], channel_multiplier=1).then_inc(sel_done, 1)
                pool.wait_ge(sel_done, k + 1)
                pool.affine_select(out=rows, in_=rows, compare_op=ALU.is_ge, fill=0.0, base=n - 1,
                                   pattern=[[n, HG]], channel_multiplier=-1).then_inc(consts, 1)
                pool.wait_ge(consts, k + 2)
            pool.memset(half[:], -0.5).then_inc(zeroed, 1)

            def norm_scale(k, b):
                pool.wait_ge(ve[k], b + 1)
                if is_first(b) and k == 0:
                    pool.wait_ge(zeroed, 3)
                pool.tensor_tensor(rstd[k][:], var_eps[k][:], half[:], ALU.pow).then_inc(rs[k], 1)

            def split(dst, v, hi_slots, lo_slot, n, done):
                stack = dst[:].rearrange("p t (h s e) -> p (t h) s e", s=TERMS, e=HD)
                heads = v.rearrange("p t (h e) -> p t h e", e=HD)
                for t in range(TT):
                    st = stack[:, t * H:(t + 1) * H]
                    a, z = hi_slots
                    pool.tensor_scalar(st[:, :, a:z + 1:z - a, :],
                                       heads[:, t].rearrange("p h (o e) -> p h o e", o=1)
                                       .to_broadcast([P, H, 2, HD]), 1.0, 0.0, ALU.mult, ALU.add)\
                        .then_inc(hi_done, 1)
                pool.wait_ge(hi_done, n + TT)
                for t in range(TT):
                    st = stack[:, t * H:(t + 1) * H]
                    ins = pool.tensor_tensor(st[:, :, lo_slot, :], heads[:, t],
                                             st[:, :, hi_slots[0], :].bitcast(F32), ALU.subtract)
                    ins.then_inc(done, 1) if t == TT - 1 else None

            def prep1(b):
                pool.wait_ge(c_in, (b + 1) * 16)
                if not is_first(b):
                    pool.wait_ge(st_done, (b - 1) * ST_PER_BATCH + 4)
                split(k_tok[0], cb[:], (0, 2), 1, b * 8, k_tok_done)
                if not is_first(b):
                    pool.wait_ge(pv_done, (b - 1) * 8 + 4)
                else:
                    pool.wait_ge(consts_v, 2)
                pool.tensor_scalar(values[0][:, :, :, 0:HD], cb[:].rearrange("p t (h e) -> p t h e", e=HD),
                                   1.0, 0.0, ALU.mult, ALU.add).then_inc(v_done, 1)
                norm_scale(0, b)
                pool.wait_ge(nm[0], (b + 1) * TT)
                split(q_tok[0], xn[:], (0, 1), 2, b * 8 + 2, q_tok_done)

            def blocks(a, b):
                for gp in range(2):
                    pool.wait_ge(st_done, b * ST_PER_BATCH + (20 * a + gp + 1))
                    for hh in range(HG):
                        pool.tensor_scalar(keys_bd[a][0:GR, 2 * gp:2 * gp + 2, hh, :],
                                           k_rows[a][:, 2 * gp:2 * gp + 2, :],
                                           head_rows[0:GR, hh:hh + 1], 0.0, ALU.mult, ALU.add)\
                            .then_inc(kbd_done, 1)

            def window(b, g):
                pool.wait_ge(st_done, b * ST_PER_BATCH + (4 + 4 * g + 4))
                p0 = probs[:, g % 2, 0, :, P:2 * P]
                p1 = probs[:, g % 2, 1, :, 0:P]
                pool.affine_select(out=p0, in_=p0, compare_op=ALU.is_ge, fill=0.0, base=0,
                                   pattern=[[0, HG], [-1, P]], channel_multiplier=1).then_inc(tri_done, 1)
                pool.affine_select(out=p1, in_=p1, compare_op=ALU.is_ge, fill=0.0, base=0,
                                   pattern=[[0, HG], [1, P]], channel_multiplier=-1).then_inc(tri_done, 1)

            def wide(v):
                return v[:].rearrange("p (o d) -> p o d", o=1).to_broadcast([P, TT, D])

            def tail_norm(b):
                norm_scale(2, b)
                pool.wait_ge(nm[2], (b + 1) * TT)
                pool.tensor_tensor(h_scaled[:], res_n[:], wide(g1_b), ALU.mult).then_inc(hs_done, 1)
                pool.wait_ge(hs_done, b + 1)
                if not is_first(b):
                    pool.wait_ge(acc_done, (b - 1) * 8 + 8)
                pool.tensor_tensor(h[:], h_scaled[:], wide(be1_b), ALU.add).then_inc(h_done, 1)

            def finish(b):
                norm_scale(3, b)
                pool.wait_ge(nm[3], (b + 1) * TT)
                pool.tensor_tensor(out_g[:], acc_n[:], wide(g2_b), ALU.mult).then_inc(og_done, 1)
                pool.wait_ge(og_done, b + 1)
                pool.tensor_tensor(out_b[:], out_g[:], wide(be2_b), ALU.add).then_inc(ob_done, 1)
                pool.wait_ge(ob_done, b + 1)
                if not is_first(b):
                    pool.wait_ge(stored, b * 16)
                pool.tensor_tensor(out_sb[:], out_b[:], x1_of(b), ALU.add).then_inc(out_done, 1)

            def prep2(b):
                norm_scale(1, b)
                pool.wait_ge(sm_done, b * SM_PER_BATCH + 20)
                if not is_first(b):
                    pool.wait_ge(st_done, (b - 1) * ST_PER_BATCH + 24)
                split(k_tok[1], qkv[:, :, D:2 * D], (0, 2), 1, b * 8 + 4, k_tok_done)
                split(q_tok[1], qkv[:, :, 0:D], (0, 1), 2, b * 8 + 6, q_tok_done)

            def prep2_late(b):
                if not is_first(b):
                    pool.wait_ge(pv_done, b * 8)
                pool.tensor_scalar(values[1][:, :, :, 0:HD],
                                   qkv[:, :, 2 * D:3 * D].rearrange("p t (h e) -> p t h e", e=HD),
                                   1.0, 0.0, ALU.mult, ALU.add).then_inc(v_done, 1)

            prep1(0)
            pool.memset(mask_above[:], 0.0).then_inc(zeroed, 1)
            pool.memset(mask_below[:], 0.0).then_inc(zeroed, 1)
            pool.memset(b2_sel[:], 0.0).then_inc(zeroed, 1)
            pool.wait_ge(zeroed, 6)
            pool.affine_select(out=mask_above[:], in_=mask_above[:], compare_op=ALU.is_ge, fill=MASKED,
                               base=0, pattern=[[0, 2], [-1, P]], channel_multiplier=1).then_inc(consts, 1)
            pool.affine_select(out=mask_below[:], in_=mask_below[:], compare_op=ALU.is_ge, fill=MASKED,
                               base=0, pattern=[[0, 2], [1, P]], channel_multiplier=-1).then_inc(consts, 1)
            pool.affine_select(out=b2_sel[:], in_=b2_sel[:], compare_op=ALU.not_equal, fill=1.0, base=0,
                               pattern=[[-1, 3]], channel_multiplier=1).then_inc(consts, 1)

            def body(i):
                if has_batch(i):
                    blocks(0, i)
                    window(i, 0)
                    window(i, 1)
                if not is_first(i):
                    tail_norm(i - 1)
                if has_batch(i):
                    window(i, 2)
                    window(i, 3)
                    prep2(i)
                    blocks(1, i)
                    prep2_late(i)
                    pool.wait_ge(nm[1], (i + 1) * TT)
                    if is_first(i):
                        pool.wait_ge(w_in, W_ALL)
                    pool.tensor_tensor(src_bo[:], src[:], wide(bo_b), ALU.add).then_inc(srcbo_done, 1)
                if has_next(i):
                    prep1(i + 1)
                if not is_first(i):
                    finish(i - 1)
            loop(pool, body)

        @block.vector
        def _(dve):
            for a in range(2):
                dve.memset(values[a][:].rearrange("p t h c -> p (t h c)"), 0.0).then_inc(consts_v, 1)
            dve.wait_ge(consts_v, 2)
            for a in range(2):
                dve.memset(values[a][:, :, :, HD:HD + 1], 1.0).then_inc(consts_v, 1)
            dve.memset(mx_hi[:].rearrange("p a b c -> p (a b c)"), 0.0).then_inc(consts_v, 1)
            dve.memset(ones_bf[:], 1.0).then_inc(consts_v, 1)

            def norm_stats(k, v, b):
                for t in range(TT):
                    dve.bn_stats(stats[k][:, t, :], v[:, t, :]).then_inc(bn[k], 1)
                dve.wait_ge(bn[k], (b + 1) * TT)
                for t in range(TT):
                    dve.bn_aggr(mean_var[k][:, t, :], stats[k][:, t, :]).then_inc(ag[k], 1)
                dve.wait_ge(ag[k], (b + 1) * TT)
                dve.tensor_scalar(var_eps[k][:], mean_var[k][:, :, 1], EPS, None, ALU.add).then_inc(ve[k], 1)

            def normalise(k, dst, v, b):
                dve.wait_ge(rs[k], b + 1)
                for t in range(TT):
                    dve.tensor_scalar(dst[:, t, :], v[:, t, :], mean_var[k][:, t, 0:1], rstd[k][:, t:t + 1],
                                      ALU.subtract, ALU.mult).then_inc(nm[k], 1)

            def norm1_stats(b):
                dve.wait_ge(x_in, (b + 1) * 16)
                norm_stats(0, xb, b)

            def norm1(b):
                if not is_first(b):
                    dve.wait_ge(q_tok_done, 2 * b - 1)
                normalise(0, xn, xb, b)

            norm1_stats(0)
            norm1(0)
            dve.wait_ge(consts, 3)
            for a in range(2):
                for g in range(G):
                    dve.tensor_copy(keys_bd[a][GR:P, g, :, :],
                                    head_rows[GR:P, :].rearrange("p (h o) -> p h o", o=1)
                                    .to_broadcast([P - GR, HG, S])).then_inc(consts_v, 1)
            dve.tensor_copy(ident_b[:], ident[:]).then_inc(consts_v, 1)
            def maxima(a, b, g, sm):
                n = b * 8 + (4 * a + g)
                par = g % 2
                for qt in range(TT):
                    for pr in range(2):
                        slot = sm.slot
                        dve.wait_ge(sm_full, sm.next() + 1)
                        dve.tensor_reduce(mx[:, par, qt, 2 * pr:2 * pr + 2],
                                          SM[slot][:].rearrange("p (h k) -> p h k", k=S), AX.X, ALU.max)\
                            .then_inc(sm_done, 1)
                dve.wait_ge(sm_done, sm.start + sm.k)
                if not (is_first(b) and a == 0 and g < 2):
                    tile = 20 * a + 4 + 4 * g - 8 if g >= 2 else 20 * a - 8 + 4 * g
                    dve.wait_ge(st_done, b * ST_PER_BATCH + (tile + 1))
                pairs = mx_hi[:, par, :, GR:GR + 2 * HG].rearrange("p t (h s) -> p t h s", s=2)
                dve.tensor_scalar(pairs[:, :, :, 0].bitcast(F32R), mx[:, par], -1.0, None, ALU.mult)\
                    .then_inc(mxh_done, 1)
                dve.wait_ge(mxh_done, n + 1)
                dve.scalar_tensor_tensor(out=pairs[:, :, :, 1].bitcast(F32R), in0=mx[:, par], scalar=-1.0,
                                         in1=pairs[:, :, :, 0], op0=ALU.mult, op1=ALU.subtract)\
                    .then_inc(mxl_done, 1)

            def divide(a, b, sm):
                for t in range(TT):
                    n = b * 4 + (2 * a + t)
                    slot = sm.slot
                    dve.wait_ge(sm_full, sm.next() + 1)
                    tile = SM[slot][:].rearrange("p (h c) -> p h c", c=VC)
                    dve.reciprocal(recip[:, t, :], tile[:, :, HD]).then_inc(recip_done, 1)
                    dve.wait_ge(recip_done, n + 1)
                    dve.tensor_tensor(att[:, t, :].rearrange("p (h e) -> p h e", e=HD), tile[:, :, 0:HD],
                                      recip[:, t, :].rearrange("p (h o) -> p h o", o=1)
                                      .to_broadcast([P, H, HD]), ALU.mult).then_inc(sm_done, 1)

            def first_residual(b, sm):
                dve.wait_ge(sm_done, sm.start + sm.k)
                dve.tensor_tensor(x1_of(b), xb[:], att[:], ALU.add).then_inc(x1_done, 1)
                dve.wait_ge(x1_done, b + 1)
                norm_stats(1, x1_of(b), b)

            def source(b):
                if not is_first(b):
                    dve.wait_ge(srcbo_done, b)
                normalise(1, src, x1_of(b), b)

            def add_bias(b, sm):
                if is_first(b):
                    dve.wait_ge(w_in, W_ALL)
                else:
                    dve.wait_ge(v_done, 2 * b)
                for t in range(TT):
                    slot = sm.slot
                    dve.wait_ge(sm_full, sm.next() + 1)
                    dve.tensor_tensor(qkv[:, t, :], SM[slot][:, 0:3 * D], bqkv[:], ALU.add)\
                        .then_inc(sm_done, 1)

            def residual2(b, sm):
                dve.wait_ge(srcbo_done, b + 1)
                for t in range(TT):
                    slot = sm.slot
                    dve.wait_ge(sm_full, sm.next() + 1)
                    dve.tensor_tensor(res[:, t, :], SM[slot][:, 0:D], src_bo[:, t, :], ALU.add)\
                        .then_inc(sm_done, 1)
                dve.wait_ge(sm_done, sm.start + sm.k)
                norm_stats(2, res, b)

            def router(b):
                dve.wait_ge(h_done, b + 1)
                if not is_first(b):
                    dve.wait_ge(acc_done, b * 8)
                r = [0]

                def step(ins):
                    r[0] += 1
                    ins.then_inc(route, 1)
                    if r[0] < ROUTE:
                        dve.wait_ge(route, b * ROUTE + r[0])

                for t in range(TT):
                    step(dve.scalar_tensor_tensor(out=junk[:, t, :], in0=h[:, t, :], scalar=1.0, in1=rw_b[:],
                                                  op0=ALU.mult, op1=ALU.mult, accum_out=key[:, t:t + 1]))
                step(dve.tensor_scalar(key_b[:], key[:], rb_b[:, 0:1], None, ALU.add))
                step(dve.tensor_copy(key_i[:], key_b[:]))
                step(dve.tensor_copy(key_f[:], key_i[:]))
                step(dve.tensor_tensor(key_gt[:], key_f[:], key_b[:], ALU.is_gt))
                step(dve.tensor_tensor(key_fl[:], key_f[:], key_gt[:], ALU.subtract))
                step(dve.tensor_copy(key_fi[:], key_fl[:]))
                step(dve.tensor_scalar(expert[:], key_fi[:], NE - 1, None, ALU.bitwise_and))
                step(dve.tensor_copy(expert_f[:], expert[:]))
                for e in range(NE):
                    step(dve.tensor_scalar(chosen[:, e, :], expert_f[:], float(e), None, ALU.is_equal))

            def add_expert(b, e):
                dve.wait_ge(down_done, b * 8 + 2 * (e + 1))
                if e == 0:
                    dve.wait_ge(route, (b + 1) * ROUTE)
                    if not is_first(b):
                        dve.wait_ge(nm[3], b * TT)
                else:
                    dve.wait_ge(acc_done, b * 8 + 2 * e)
                base = h if e == 0 else acc
                for t in range(TT):
                    ins = dve.scalar_tensor_tensor(out=acc[:, t, :], in0=Y[:, t * D:(t + 1) * D],
                                                   scalar=chosen[:, e, t:t + 1], in1=base[:, t, :],
                                                   op0=ALU.mult, op1=ALU.add)
                    ins.then_inc(acc_done, 1)

            def norm4(b):
                dve.wait_ge(acc_done, b * 8 + 8)
                norm_stats(3, acc, b)

            def setup_b2():
                r = [0]

                def step(ins):
                    r[0] += 1
                    ins.then_inc(b2_step, 1)
                    dve.wait_ge(b2_step, r[0])

                dve.wait_ge(wf_in, WF_ALL)
                dve.wait_ge(consts, 6)
                step(dve.tensor_copy(b2_part[:, 0, :], b2_3[:]))
                step(dve.tensor_tensor(b2_left[:, 0, :], b2_3[:], b2_part[:, 0, :], ALU.subtract))
                step(dve.tensor_copy(b2_part[:, 1, :], b2_left[:, 0, :]))
                step(dve.tensor_tensor(b2_left[:, 1, :], b2_left[:, 0, :], b2_part[:, 1, :], ALU.subtract))
                step(dve.tensor_copy(b2_part[:, 2, :], b2_left[:, 1, :]))
                step(dve.tensor_scalar(b2_pick[:, 0, :], b2_part[:, 0, :], b2_sel[:, 0:1], None, ALU.mult))
                step(dve.scalar_tensor_tensor(out=b2_pick[:, 1, :], in0=b2_part[:, 1, :],
                                              scalar=b2_sel[:, 1:2], in1=b2_pick[:, 0, :],
                                              op0=ALU.mult, op1=ALU.add))
                step(dve.scalar_tensor_tensor(out=b2_bf[:].rearrange("r e d -> r (e d)"),
                                              in0=b2_part[:, 2, :], scalar=b2_sel[:, 2:3],
                                              in1=b2_pick[:, 1, :], op0=ALU.mult, op1=ALU.add))

            def body(i):
                sm = Turn(sm_start(i))
                live, tail = has_batch(i), not is_first(i)
                if tail:
                    divide(1, i - 1, sm)
                if live:
                    maxima(0, i, 0, sm)
                    maxima(0, i, 1, sm)
                if tail:
                    residual2(i - 1, sm)
                if live:
                    maxima(0, i, 2, sm)
                if tail:
                    normalise(2, res_n, res, i - 1)
                if live:
                    maxima(0, i, 3, sm)
                if tail:
                    router(i - 1)
                if live:
                    divide(0, i, sm)
                    first_residual(i, sm)
                    source(i)
                if tail:
                    add_expert(i - 1, 0)
                if live:
                    add_bias(i, sm)
                if tail:
                    add_expert(i - 1, 1)
                if is_first(i):
                    setup_b2()
                if live:
                    maxima(1, i, 0, sm)
                if tail:
                    add_expert(i - 1, 2)
                if has_next(i):
                    norm1_stats(i + 1)
                if live:
                    maxima(1, i, 1, sm)
                if has_next(i):
                    norm1(i + 1)
                if live:
                    maxima(1, i, 2, sm)
                if live:
                    maxima(1, i, 3, sm)
                if tail:
                    add_expert(i - 1, 3)
                    norm4(i - 1)
                    normalise(3, acc_n, acc, i - 1)
            loop(dve, body)

        @block.scalar
        def _(act):
            def evacuate_stacks(a, b, st):
                for k in range(4):
                    slot = st.slot
                    act.wait_ge(st_full, st.next() + 1)
                    dst = k_rows[a][:, 2 * k:2 * k + 2, :] if k < 2 else \
                        q_rows[a][0:GR, 2 * (k - 2):2 * (k - 2) + 2, :]
                    act.copy(dst, ST[slot][0:GR, :].rearrange("p (g s) -> p g s", s=S)).then_inc(st_done, 1)

            def small(dst, src_ap, mb):
                act.wait_ge(mb_full, mb.next() + 1)
                act.copy(dst, src_ap).then_inc(mb_done, 1)

            def exps(a, b, g, st, mb):
                small(q_rows[a][GR:P, g, :], MB[GR:P, 0:S], mb)
                n = b * 8 + (4 * a + g)
                if not (isinstance(n, int) and n < 2):
                    act.wait_ge(pv_done, n - 1)
                for kb in range(TT):
                    for pr in range(2):
                        slot = st.slot
                        act.wait_ge(st_full, st.next() + 1)
                        act.activation(probs[:, g % 2, kb, 2 * pr:2 * pr + 2, :],
                                       ST[slot][:].rearrange("p (h q) -> p h q", q=S), ACT.Exp,
                                       scale=SCALE2 if a else 1.0).then_inc(st_done, 1)

            def evacuate_heads(a, b, k):
                act.wait_ge(pv_done, b * 8 + (4 * a + 2 * k + 2))
                act.copy(heads_t[:, 2 * k:2 * k + 2, :], PO[:].rearrange("p (g s) -> p g s", s=S))\
                    .then_inc(po_done, 1)

            def relu(b, u):
                if u >= 2:
                    act.wait_ge(down_done, b * 8 + (u - 1))
                act.wait_ge(up_full, b * 8 + (u + 1))
                for c in range(2):
                    ins = act.activation(hid[:, u % 2, c, :], UP[:, c * S:(c + 1) * S], ACT.Relu,
                                         bias=b1_cols[:, 2 * u + c:2 * u + c + 1])
                    ins.then_inc(up_done, 1) if c else None

            def body(i):
                st = Turn(i * ST_PER_BATCH)
                mb = Turn(mb_start(i))
                live, tail = has_batch(i), not is_first(i)
                if live:
                    evacuate_stacks(0, i, st)
                if tail:
                    small(att_t[:], MB[:, 0:S], mb)
                if live:
                    exps(0, i, 0, st, mb)
                    exps(0, i, 1, st, mb)
                    exps(0, i, 2, st, mb)
                if tail:
                    small(h_t[:], MB[:, 0:S], mb)
                if live:
                    evacuate_heads(0, i, 0)
                    exps(0, i, 3, st, mb)
                if tail:
                    relu(i - 1, 0)
                if live:
                    evacuate_heads(0, i, 1)
                if tail:
                    relu(i - 1, 1)
                    relu(i - 1, 2)
                if live:
                    small(src_t[:], MB[:, 0:S], mb)
                if tail:
                    relu(i - 1, 3)
                    relu(i - 1, 4)
                if live:
                    evacuate_stacks(1, i, st)
                if tail:
                    relu(i - 1, 5)
                if tail:
                    relu(i - 1, 6)
                if live:
                    exps(1, i, 0, st, mb)
                if tail:
                    relu(i - 1, 7)
                if live:
                    exps(1, i, 1, st, mb)
                    exps(1, i, 2, st, mb)
                    evacuate_heads(1, i, 0)
                    exps(1, i, 3, st, mb)
                    evacuate_heads(1, i, 1)
                if is_first(i):
                    small(b1_cols[:], MB[:, 0:NE * FC], mb)
            loop(act, body)

        @block.tensor
        def _(pe):
            def ring(free, n):
                if not (isinstance(n, int) and n < 2):
                    pe.wait_ge(free, n - 1)

            def single(free, n):
                if not (isinstance(n, int) and n < 1):
                    pe.wait_ge(free, n)

            def stacks(a, b, st):
                pe.wait_ge(k_tok_done, 2 * b + (a + 1))
                for k in range(4):
                    if k == 2:
                        pe.wait_ge(q_tok_done, 2 * b + (a + 1))
                    tok = (k_tok if k < 2 else q_tok)[a]
                    slot = st.slot
                    ring(st_done, st.next())
                    for g in range(2):
                        for t in range(TT):
                            c = (2 * (k % 2) + g) * GR
                            ins = pe.transpose(ST[slot][0:GR, g * S + t * P:g * S + (t + 1) * P],
                                               tok[:, t, c:c + GR].bitcast(F32), ident[:])
                    ins.then_inc(st_full, 1)

            def scores(a, b, g, sm):
                pe.wait_ge(st_done, b * ST_PER_BATCH + (20 * a + 3 + g // 2))
                for qt in range(TT):
                    for pr in range(2):
                        if qt == 0:
                            pe.wait_ge(kbd_done, b * 16 + (8 * a + 4 * (g // 2) + 2 * pr + 2))
                        slot = sm.slot
                        ring(sm_done, sm.next())
                        ins = pe.matmul(SM[slot][:], q_rows[a][0:GR, g, qt * P:(qt + 1) * P],
                                        keys_bd[a][0:GR, g, 2 * pr:2 * pr + 2, :],
                                        start=True, stop=True)
                        if a == 0:
                            kt = 1 - qt
                            tri = SM[slot][:].rearrange("p (h k) -> p h k", k=S)[:, :, kt * P:(kt + 1) * P]
                            ins = pe.matmul(tri, ident_b[:], (mask_above, mask_below)[qt][:],
                                            start=False, stop=True, skip_group_check=True)
                        ins.then_inc(sm_full, 1)

            def key_major(a, b, g, st, mb):
                n = b * 8 + (4 * a + g)
                pe.wait_ge(mxl_done, n + 1)
                m = mb.next()
                single(mb_done, m)
                for qt in range(TT):
                    ins = pe.transpose(MB[:, qt * P:(qt + 1) * P], mx_hi[:, g % 2, qt, :], ident[:])
                ins.then_inc(mb_full, 1)
                pe.wait_ge(mb_done, m + 1)
                for kb in range(TT):
                    for pr in range(2):
                        slot = st.slot
                        ring(st_done, st.next())
                        for j in range(2):
                            hh = 2 * pr + j
                            ins = pe.matmul(ST[slot][:, j * S:(j + 1) * S],
                                            keys_bd[a][:, g, hh, kb * P:(kb + 1) * P],
                                            q_rows[a][:, g, :], start=True, stop=True)
                        ins.then_inc(st_full, 1)

            def weigh(a, b, g):
                if a == 0:
                    pe.wait_ge(tri_done, b * 8 + (2 * g + 2))
                pe.wait_ge(st_done, b * ST_PER_BATCH + (20 * a + 4 + 4 * g + 4))
                if g == 0:
                    pe.wait_ge(v_done, 2 * b + (a + 1))
                if g % 2 == 0:
                    single(po_done, b * 4 + (2 * a + g // 2))
                for kb in range(TT):
                    for hh in range(HG):
                        ins = pe.matmul(PO[VC * hh:VC * (hh + 1), (g % 2) * S:(g % 2 + 1) * S],
                                        values[a][:, kb, HG * g + hh, :], probs[:, g % 2, kb, hh, :],
                                        start=(kb == 0), stop=(kb == TT - 1))
                ins.then_inc(pv_done, 1)

            def attention(a, b, st, sm, mb, between):
                for s in range(G + 2):
                    if s < G:
                        scores(a, b, s, sm)
                    between(s)
                    if 1 <= s <= G:
                        key_major(a, b, s - 1, st, mb)
                    if s >= 2:
                        weigh(a, b, s - 2)

            def back(a, b, sm):
                pe.wait_ge(po_done, b * 4 + (2 * a + 2))
                for t in range(TT):
                    slot = sm.slot
                    ring(sm_done, sm.next())
                    for g in range(G):
                        ins = pe.transpose(SM[slot][:, g * P:(g + 1) * P], heads_t[:, g, t * P:(t + 1) * P],
                                           ident[:])
                    ins.then_inc(sm_full, 1)

            def turn_small(v, mb):
                single(mb_done, mb.next())
                for t in range(TT):
                    ins = pe.transpose(MB[:, t * P:(t + 1) * P], v[:, t, :], ident[:])
                ins.then_inc(mb_full, 1)

            def project(lhs, rhs, n, sm, mb):
                pe.wait_ge(mb_done, mb.start + mb.k)
                for t in range(TT):
                    slot = sm.slot
                    ring(sm_done, sm.next())
                    pe.matmul(SM[slot][:, 0:n], lhs[:, t * P:(t + 1) * P], rhs[:], start=True, stop=True)\
                        .then_inc(sm_full, 1)

            def up(b, u):
                single(up_done, b * 8 + u)
                e = u // 2
                for c in range(2):
                    f = (2 * (u % 2) + c) * P
                    ins = pe.matmul(UP[:, c * S:(c + 1) * S], w1[:, e, f:f + P], h_t[:], start=True, stop=True)
                ins.then_inc(up_full, 1)

            def down(b, u):
                e = u // 2
                if u % 2 == 0:
                    single(acc_done, b * 8 + 2 * e)
                    pe.matmul(Y[:, 0:TT * D], ones_bf[:],
                              b2_bf[:, e, :].rearrange("r (o d) -> r o d", o=1).to_broadcast([TERMS, TT, D]),
                              start=True, stop=False, skip_group_check=True)
                pe.wait_ge(up_done, b * 8 + (u + 1))
                for c in range(2):
                    for t in range(TT):
                        ins = pe.matmul(Y[:, t * D:(t + 1) * D], hid[:, u % 2, c, t * P:(t + 1) * P],
                                        w2[:, e, 2 * (u % 2) + c, :], start=False,
                                        stop=(u % 2 == 1 and c == 1), skip_group_check=True)
                        if c == 1 and t == TT - 1:
                            ins.then_inc(down_done, 1)

            def feed(b, q):
                if q > 0:
                    down(b, q - 1)
                if q < 8:
                    up(b, q)

            def body(i):
                st, sm, mb = Turn(i * ST_PER_BATCH), Turn(sm_start(i)), Turn(mb_start(i))
                live, tail = has_batch(i), not is_first(i)
                if is_first(i):
                    pe.wait_ge(consts, 1)
                if live:
                    stacks(0, i, st)
                if is_first(i):
                    pe.wait_ge(consts, 6)
                    pe.wait_ge(consts_v, CONST_V)
                if tail:
                    back(1, i - 1, sm)

                def part1(s):
                    if not tail:
                        return
                    if s == 0:
                        pe.wait_ge(sm_done, sm_start(i) + 2)
                        turn_small(att, mb)
                    if s == 1:
                        project(att_t, wo, D, sm, mb)
                    if s == 4:
                        pe.wait_ge(h_done, i)
                        turn_small(h, mb)
                        pe.wait_ge(mb_done, mb.start + mb.k)
                    if s == 5:
                        feed(i - 1, 0)
                        feed(i - 1, 1)

                if live:
                    attention(0, i, st, sm, mb, part1)
                    back(0, i, sm)
                else:
                    for s in range(6):
                        part1(s)
                if tail:
                    feed(i - 1, 2)
                if live:
                    pe.wait_ge(nm[1], (i + 1) * TT)
                    turn_small(src, mb)
                if tail:
                    feed(i - 1, 3)
                if live:
                    if is_first(i):
                        pe.wait_ge(w_in, W_ALL)
                    project(src_t, wqkv, 3 * D, sm, mb)
                if tail:
                    feed(i - 1, 4)
                if live:
                    stacks(1, i, st)
                if tail:
                    feed(i - 1, 5)

                def part2(s):
                    if tail and s in (0, 2, 3):
                        feed(i - 1, {0: 6, 2: 7, 3: 8}[s])

                if live:
                    attention(1, i, st, sm, mb, part2)
                else:
                    for s in range(G):
                        part2(s)
                if is_first(i):
                    pe.wait_ge(wf_in, WF_ALL)
                    single(mb_done, mb.next())
                    pe.transpose(MB[:, 0:NE * FC], b1_rows[:], ident[0:NE * FC, 0:NE * FC]).then_inc(mb_full, 1)
                    pe.wait_ge(b2_step, 8)
            loop(pe, body)


_INS = ["x", "ctx_1024"] + ["L0_ffn_" + n for n in (
    "Wq", "bq", "Wk", "bk", "Wv", "bv", "Wo", "bo", "router_w", "router_b", "W1", "b1", "W2", "b2",
    "ln1_g", "ln1_b", "ln2_g", "ln2_b")]


def kernel(**inputs):
    import concourse.bacc as bacc
    from concourse.bass_utils import run_bass_kernel_spmd

    nc = bacc.Bacc("TRN2", target_bir_lowering=False, num_devices=1)
    arrays, args = {}, []
    for name in _INS:
        a = np.ascontiguousarray(inputs[name])
        arrays[f"in_{name}"] = a
        args.append(nc.dram_tensor(f"in_{name}", a.shape, mybir.dt.from_np(a.dtype), kind="ExternalInput").ap())
    args.append(nc.dram_tensor("out_0", (B, S, D), F32, kind="ExternalOutput").ap())
    build(nc, *args)
    r = run_bass_kernel_spmd(nc, [arrays], core_ids=[0])
    return r.results[0]["out_0"]
```

```python
from contextlib import ExitStack

import numpy as np
import concourse.bass as bass
from concourse import mybir

ALU = mybir.AluOpType
ACT = mybir.ActivationFunctionType
AX = mybir.AxisListType
F32 = mybir.dt.float32
F32R = mybir.dt.float32r
BF16 = mybir.dt.bfloat16
I32 = mybir.dt.int32

P = 128
B, S = 4, 256
TT = S // P
D = 128
H = 16
HD = D // H
G = 4
HG = H // G
TERMS = 3
HR = TERMS * HD
GR = HG * HR
VC = 32
NE = 4
FF = 512
FC = FF // P
EPS = 1e-5
MASKED = -1.0e30
SCALE2 = float(HD) ** -0.5

LAST_STEP = 46

SEQ = [(0, 0), (0, 1), (0, 2), (1, 0), (0, 3), (1, 1), (1, 2), (1, 3)]
N = len(SEQ)
JOBS = G * N
FIRST = [G * SEQ.index((0, b)) for b in range(B)]
SECOND = [G * SEQ.index((1, b)) for b in range(B)]


def place_stacks():
    at = {}
    for n, (a, b) in enumerate(SEQ):
        start = G * n
        if n == 0:
            spots = [(-1, 0), (-1, 1), (-1, 2), (-1, 3)]
        elif n == 1:
            spots = [(1, 1), (1, 3), (2, 1), (2, 3)]
        elif a == 1 and start - FIRST[b] <= 12:
            spots = [(start - 1, 0), (start - 1, 1), (start - 1, 2), (start - 1, 3)]
        else:
            spots = [(start - 3, 1), (start - 3, 3), (start - 2, 1), (start - 2, 3)]
        for k, spot in enumerate(spots):
            at.setdefault(spot, []).append((n, k))
    return at


def place_experts():
    at = {}
    spots = {
        0: [(23 + q, 2) for q in range(8)] + [(31, 0)],
        1: [(31 + q // 2, 1 + 2 * (q % 2)) for q in range(9)],
        2: [(35 + (q + 1) // 2, 1 + 2 * ((q + 1) % 2)) for q in range(9)],
        3: [(39 + (q + 2) // 2, 1 + 2 * (q % 2)) for q in range(9)],
    }
    for b, of_batch in spots.items():
        for q, spot in enumerate(of_batch):
            at.setdefault(spot, []).append((b, q))
    return at


STACKS_AT = place_stacks()
EXPERTS_AT = place_experts()


def batch_at(starts, step, offset):
    return starts.index(step - offset) if step - offset in starts else None


def number(uses):
    return {use: k for k, use in enumerate(uses)}


BACK, SRC_T, PROJECT = 7, 9, 10
ATT_T, OUT_PROJECT, H_T = 8, 9, 11


def st_uses():
    for s in range(-1, LAST_STEP):
        for slot in range(4):
            yield from (("stacks", n, k) for n, k in STACKS_AT.get((s, slot), []))
            if 0 <= s - 2 < JOBS:
                yield ("scores", s - 2, slot)


def sm_uses():
    for s in range(LAST_STEP):
        for slot in range(4):
            if s < JOBS:
                yield ("scores", s, slot)
            if slot >= 2:
                n, g = divmod(s - BACK, G)
                if g == 0 and 0 <= n < N:
                    yield ("back", n, slot - 2)
            else:
                if (b := batch_at(FIRST, s, PROJECT)) is not None:
                    yield ("project", b, slot)
                if (b := batch_at(SECOND, s, OUT_PROJECT)) is not None:
                    yield ("out_project", b, slot)


def mb_uses():
    for s in range(LAST_STEP):
        for slot in range(4):
            if slot == 0 and (b := batch_at(FIRST, s, SRC_T)) is not None:
                yield ("src", b)
            if slot == 0 and (b := batch_at(SECOND, s, H_T)) is not None:
                yield ("h", b)
            if slot == 1 and 0 <= s - 1 < JOBS:
                yield ("maxima", s - 1)
            if slot == 2 and (b := batch_at(SECOND, s, ATT_T)) is not None:
                yield ("att", b)
            if slot == 2 and s == B1_STEP:
                yield ("b1",)


B1_STEP = 14
FIRST_JOBS = [j for j in range(JOBS) if SEQ[j // G][0] == 0]
STEP_OF_STACK = {use: spot[0] for spot, of in STACKS_AT.items() for use in of}
HIGH_STEP = {n: FIRST[b] + PROJECT if a else G * n - 5 for n, (a, b) in enumerate(SEQ) if n >= 2}


def later(spot, slots):
    s, slot = spot
    return s + (slot + slots) // 4, (slot + slots) % 4


def place_relus():
    at = {}
    for spot, parts in EXPERTS_AT.items():
        for b, q in parts:
            if q < 8:
                at.setdefault(later(spot, 1), []).append((b, q))
    return at


def place_sums():
    at = {}
    for spot, parts in EXPERTS_AT.items():
        for b, q in parts:
            if q and q % 2 == 0:
                at.setdefault(later(spot, 1), []).append((b, q // 2 - 1))
    return at


RELU_AT, EXPERT_SUM_AT = place_relus(), place_sums()
FINISH_STEP = [next(s for (s, _), of in EXPERT_SUM_AT.items() if (b, NE - 1) in of) for b in range(B)]
ST_USE, SM_USE, MB_USE = number(st_uses()), number(sm_uses()), number(mb_uses())


def build(nc, x, ctx_in, Wq, bq, Wk, bk, Wv, bv, Wo, bo, rw, rb, W1, b1, W2, b2, g1, be1, g2, be2, out):
    with ExitStack() as ctx:
        def sb(name, shape, dt=F32):
            return ctx.enter_context(nc.sbuf_tensor(name, shape, dt))

        def bank(name):
            return ctx.enter_context(nc.psum_tensor(name, [P, 512], F32))

        def sem(name):
            return ctx.enter_context(nc.semaphore(name))

        xb = [sb(f"xb{b}", [P, TT, D]) for b in range(B)]
        cb = [sb(f"cb{b}", [P, TT, D]) for b in range(B)]
        wqkv = sb("wqkv", [P, 3 * D])
        bqkv = sb("bqkv", [P, 3 * D])
        wo = sb("wo", [P, D])
        bo_b = sb("bo_b", [P, D])
        rw_b = sb("rw_b", [P, D])
        rb_b = sb("rb_b", [P, 1])
        g1_b = sb("g1_b", [P, D])
        be1_b = sb("be1_b", [P, D])
        g2_b = sb("g2_b", [P, D])
        be2_b = sb("be2_b", [P, D])
        w1 = sb("w1", [P, NE, FF])
        w2 = sb("w2", [P, NE, FC, D])
        b1_rows = sb("b1_rows", [NE * FC, P])
        b1_cols = sb("b1_cols", [P, NE * FC])
        b2_3 = sb("b2_3", [TERMS, NE * D])
        ident = sb("ident", [P, P])
        ident_b = sb("ident_b", [P, P], BF16)
        mask_above = sb("mask_above", [P, 2, P], BF16)
        mask_below = sb("mask_below", [P, 2, P], BF16)
        head_rows = sb("head_rows", [P, HG])
        half = sb("half", [P, TT])
        b2_part = sb("b2_part", [TERMS, 3, NE * D], BF16)
        b2_left = sb("b2_left", [TERMS, 2, NE * D])
        b2_sel = sb("b2_sel", [TERMS, 3])
        b2_pick = sb("b2_pick", [TERMS, 3, NE * D])
        b2_bf = sb("b2_bf", [TERMS, NE, D], BF16)
        ones_bf = sb("ones_bf", [TERMS, P], BF16)
        stats = [sb(f"stats{k}", [P, TT, 6]) for k in range(4)]
        mean_var = [sb(f"mean_var{k}", [P, TT, 2]) for k in range(4)]
        var_eps = [sb(f"var_eps{k}", [P, TT]) for k in range(4)]
        rstd = [sb(f"rstd{k}", [P, TT]) for k in range(4)]
        xn = [sb(f"xn{k}", [P, TT, D]) for k in range(2)]
        q_tok = [sb(f"q_tok{a}", [P, TT, H * HR], F32R) for a in range(3)]
        k_tok = [sb(f"k_tok{a}", [P, TT, H * HR], F32R) for a in range(3)]
        q_rows = [sb(f"q_rows{a}", [P, G, S], F32R) for a in range(3)]
        k_rows = [sb(f"k_rows{a}", [GR, G, S]) for a in range(3)]
        keys_bd = [sb(f"keys_blockdiag{a}", [P, G, HG, S], F32R) for a in range(3)]
        values = [sb(f"values{a}", [P, TT, H, VC]) for a in range(3)]
        mx = sb("mx", [P, 2, TT, HG])
        mx_hi = sb("mx_hi", [P, 2, TT, P])
        probs = sb("probs", [P, 2, TT, HG, S])
        heads_t = sb("heads_t", [P, G, S])
        recip = sb("recip", [P, TT, H])
        att = sb("att", [P, TT, D])
        x1 = [sb(f"x1_{b}", [P, TT, D]) for b in range(B)]
        src = sb("src", [P, TT, D])
        src_bo = [sb(f"src_bo{b}", [P, TT, D]) for b in range(B)]
        src_t = sb("src_t", [P, S])
        qkv = sb("qkv", [P, TT, 3 * D])
        att_t = sb("att_t", [P, S])
        res = sb("res", [P, TT, D])
        res_n = sb("res_n", [P, TT, D])
        h_scaled = sb("h_scaled", [P, TT, D])
        h = sb("h", [P, TT, D])
        h_t = [sb(f"h_t{k}", [P, S]) for k in range(2)]
        junk = sb("junk", [P, TT, D])
        key = sb("key", [P, TT])
        key_b = sb("key_b", [P, TT])
        key_i = sb("key_i", [P, TT], I32)
        key_f = sb("key_f", [P, TT])
        key_gt = sb("key_gt", [P, TT])
        key_fl = sb("key_fl", [P, TT])
        key_fi = sb("key_fi", [P, TT], I32)
        expert = sb("expert", [P, TT], I32)
        expert_f = sb("expert_f", [P, TT])
        chosen = sb("chosen", [P, 2, NE, TT])
        hid = sb("hid", [P, 2, 2, S])
        acc = sb("acc", [P, TT, D])
        acc_n = sb("acc_n", [P, TT, D])
        out_g = sb("out_g", [P, TT, D])
        out_b = sb("out_b", [P, TT, D])
        out_sb = sb("out_sb", [P, TT, D])
        ST = [bank(f"ST{k}") for k in range(2)]
        SM = [bank(f"SM{k}") for k in range(2)]
        PO = bank("PO")
        Y = bank("Y")
        UP = bank("UP")
        MB = bank("MB")
        x_in = [sem(f"x_in{b}") for b in range(B)]
        c_in = [sem(f"c_in{b}") for b in range(B)]
        w_in, wf_in = sem("w_in"), sem("wf_in")
        consts = sem("consts")
        consts_v = sem("consts_v")
        ident_b_done = sem("ident_b_done")
        zeroed = sem("zeroed")
        sel_done = sem("sel_done")
        b2_step = sem("b2_step")
        st_full, st_done = sem("st_full"), sem("st_done")
        sm_full, sm_done = sem("sm_full"), sem("sm_done")
        mb_full, mb_done = sem("mb_full"), sem("mb_done")
        po_done = sem("po_done")
        up_full, up_done = sem("up_full"), sem("up_done")
        pv_done = sem("pv_done")
        down_done = sem("down_done")
        bn = [sem(f"bn{k}") for k in range(4)]
        ag = [sem(f"ag{k}") for k in range(4)]
        ve = [sem(f"ve{k}") for k in range(4)]
        rs = [sem(f"rs{k}") for k in range(4)]
        nm = [sem(f"nm{k}") for k in range(4)]
        k_hi_done, q_hi_done = sem("k_hi_done"), sem("q_hi_done")
        q_tok_done, k_tok_done = sem("q_tok_done"), sem("k_tok_done")
        v_done = sem("v_done")
        kbd_done = sem("kbd_done")
        mx_done = sem("mx_done")
        mxh_done = sem("mxh_done")
        mxl_done = sem("mxl_done")
        tri_done = sem("tri_done")
        recip_done, att_done = sem("recip_done"), sem("att_done")
        x1_done = sem("x1_done")
        srcbo_done = sem("srcbo_done")
        hs_done, h_done = sem("hs_done"), sem("h_done")
        route = sem("route")
        acc_done = sem("acc_done")
        og_done, ob_done = sem("og_done"), sem("ob_done")
        out_done, stored = sem("out_done"), sem("stored")

        block = ctx.enter_context(nc.Block())

        xr = x.rearrange("b (t p) d -> b p t d", p=P)
        cr = ctx_in.rearrange("b (t p) d -> b p t d", p=P)
        outr = out.rearrange("b (t p) d -> b p t d", p=P)
        W_ALL, WF_ALL = 16 * 14, 16 * 4
        CONST_V = 7 + 3
        ROUTE = TT + 8 + NE

        def row(v):
            return v.rearrange("(a d) -> a d", a=1).to_broadcast([P, D])

        def by_head(v):
            return v.rearrange("p t (h e) -> p t h e", e=HD)

        def wide(v):
            return v[:].rearrange("p (o d) -> p o d", o=1).to_broadcast([P, TT, D])

        def operands(n):
            a, b = SEQ[n]
            if a == 0:
                return cb[b][:], xn[b % 2][:], cb[b][:]
            return qkv[:, :, D:2 * D], qkv[:, :, 0:D], qkv[:, :, 2 * D:3 * D]

        @block.sync
        def _(sp):
            for b in range(2):
                sp.dma_start(xb[b][:], xr[b]).then_inc(x_in[b], 16)
            for k, w in enumerate((Wq, Wk, Wv)):
                sp.dma_start(wqkv[:, k * D:(k + 1) * D], w).then_inc(w_in, 16)
            for k, v in enumerate((bq, bk, bv)):
                sp.dma_start(bqkv[:, k * D:(k + 1) * D], row(v)).then_inc(w_in, 16)
            sp.dma_start(wo[:], Wo).then_inc(w_in, 16)
            for t, v in ((bo_b, bo), (g1_b, g1), (be1_b, be1), (g2_b, g2), (be2_b, be2)):
                sp.dma_start(t[:], row(v)).then_inc(w_in, 16)
            sp.dma_start(rw_b[:], row(rw.rearrange("d a -> (d a)"))).then_inc(w_in, 16)
            sp.dma_start(rb_b[:], rb.rearrange("(a d) -> a d", a=1).to_broadcast([P, 1])).then_inc(w_in, 16)
            for b in range(2, B):
                sp.dma_start(cb[b][:], cr[b]).then_inc(c_in[b], 16)
                sp.dma_start(xb[b][:], xr[b]).then_inc(x_in[b], 16)
            sp.dma_start(b1_rows[:], b1.rearrange("e (c p) -> (e c) p", p=P)).then_inc(wf_in, 16)
            sp.dma_start(b2_3[:], b2.rearrange("e d -> (e d)").rearrange("(a n) -> a n", a=1)
                         .to_broadcast([TERMS, NE * D])).then_inc(wf_in, 16)
            sp.dma_start(w1[:], W1.rearrange("e d f -> d e f")).then_inc(wf_in, 16)
            sp.dma_start(w2[:], W2.rearrange("e (c p) d -> p e c d", p=P)).then_inc(wf_in, 16)
            for b in range(B):
                sp.wait_ge(out_done, b + 1)
                sp.dma_start(outr[b], out_sb[:]).then_inc(stored, 16)
            sp.wait_ge(stored, 16 * B)

        @block.gpsimd
        def _(pool):
            pool.memset(ident[:], 0.0).then_inc(zeroed, 1)
            pool.memset(head_rows[:], 1.0).then_inc(zeroed, 1)
            pool.memset(half[:], -0.5).then_inc(zeroed, 1)
            pool.wait_ge(zeroed, 3)
            pool.affine_select(out=ident[:], in_=ident[:], compare_op=ALU.not_equal, fill=1.0, base=0,
                               pattern=[[-1, P]], channel_multiplier=1).then_inc(consts, 1)

            def norm_scale(k, b):
                pool.wait_ge(ve[k], b + 1)
                pool.tensor_tensor(rstd[k][:], var_eps[k][:], half[:], ALU.pow).then_inc(rs[k], 1)

            def low_part(dst, v, lo_slot, hi_slot, done):
                stack = dst[:].rearrange("p t (h s e) -> p t h s e", s=TERMS, e=HD)
                pool.tensor_tensor(stack[:, :, :, lo_slot, :], by_head(v),
                                   stack[:, :, :, hi_slot, :].bitcast(F32), ALU.subtract).then_inc(done, 1)

            def keys_low(n):
                pool.wait_ge(k_hi_done, n + 1)
                low_part(k_tok[n % 3], operands(n)[0], 1, 0, k_tok_done)

            def queries_low(n):
                pool.wait_ge(q_hi_done, n + 1)
                low_part(q_tok[n % 3], operands(n)[1], 2, 0, q_tok_done)

            def blocks(n, gp):
                pool.wait_ge(st_done, ST_USE[("stacks", n, gp)] + 1)
                for hh in range(HG):
                    pool.tensor_scalar(keys_bd[n % 3][0:GR, 2 * gp:2 * gp + 2, hh, :],
                                       k_rows[n % 3][:, 2 * gp:2 * gp + 2, :],
                                       head_rows[0:GR, hh:hh + 1], 0.0, ALU.mult, ALU.add)\
                        .then_inc(kbd_done, 1)

            def window(job, kb):
                pool.wait_ge(st_done, ST_USE[("scores", job, 2 * kb + 1)] + 1)
                sign = 1 if kb == 0 else -1
                p = probs[:, job % 2, kb, :, P:2 * P] if kb == 0 else probs[:, job % 2, kb, :, 0:P]
                pool.affine_select(out=p, in_=p, compare_op=ALU.is_ge, fill=0.0, base=0,
                                   pattern=[[0, HG], [-sign, P]], channel_multiplier=sign).then_inc(tri_done, 1)

            def h_of(b):
                pool.wait_ge(nm[2], (b + 1) * TT)
                pool.tensor_tensor(h_scaled[:], res_n[:], wide(g1_b), ALU.mult).then_inc(hs_done, 1)
                pool.wait_ge(hs_done, b + 1)
                if b:
                    pool.wait_ge(acc_done, (b - 1) * 8 + 2)
                pool.tensor_tensor(h[:], h_scaled[:], wide(be1_b), ALU.add).then_inc(h_done, 1)

            def finish(b):
                norm_scale(3, b)
                pool.wait_ge(nm[3], (b + 1) * TT)
                pool.tensor_tensor(out_g[:], acc_n[:], wide(g2_b), ALU.mult).then_inc(og_done, 1)
                pool.wait_ge(og_done, b + 1)
                pool.tensor_tensor(out_b[:], out_g[:], wide(be2_b), ALU.add).then_inc(ob_done, 1)
                pool.wait_ge(ob_done, b + 1)
                if b:
                    pool.wait_ge(stored, b * 16)
                pool.tensor_tensor(out_sb[:], out_b[:], x1[b][:], ALU.add).then_inc(out_done, 1)

            def source_bias(b):
                pool.wait_ge(nm[1], (b + 1) * TT)
                pool.tensor_tensor(src_bo[b][:], src[:], wide(bo_b), ALU.add).then_inc(srcbo_done, 1)

            keys_low(0)
            norm_scale(0, 0)
            edges = ((0, GR, HR), (GR, P, 2))
            pool.wait_ge(k_tok_done, 1)
            pool.wait_ge(rs[0], 1)
            for k, (lo, hi, n) in enumerate(edges):
                rows = head_rows[lo:hi, :]
                pool.affine_select(out=rows, in_=rows, compare_op=ALU.is_ge, fill=0.0, base=0,
                                   pattern=[[-n, HG]], channel_multiplier=1).then_inc(sel_done, 1)
                pool.wait_ge(sel_done, k + 1)
                pool.affine_select(out=rows, in_=rows, compare_op=ALU.is_ge, fill=0.0, base=n - 1,
                                   pattern=[[n, HG]], channel_multiplier=-1).then_inc(consts, 1)
                pool.wait_ge(consts, k + 2)
            queries_low(0)
            norm_scale(0, 1)
            blocks(0, 0)
            pool.memset(mask_above[:], 0.0).then_inc(zeroed, 1)
            pool.memset(mask_below[:], 0.0).then_inc(zeroed, 1)
            pool.wait_ge(zeroed, 5)
            pool.affine_select(out=mask_above[:], in_=mask_above[:], compare_op=ALU.is_ge, fill=MASKED,
                               base=0, pattern=[[0, 2], [-1, P]], channel_multiplier=1).then_inc(consts, 1)
            pool.affine_select(out=mask_below[:], in_=mask_below[:], compare_op=ALU.is_ge, fill=MASKED,
                               base=0, pattern=[[0, 2], [1, P]], channel_multiplier=-1).then_inc(consts, 1)
            blocks(0, 1)
            keys_low(1)
            queries_low(1)
            pool.memset(b2_sel[:], 0.0).then_inc(zeroed, 1)
            pool.wait_ge(zeroed, 6)
            pool.affine_select(out=b2_sel[:], in_=b2_sel[:], compare_op=ALU.not_equal, fill=1.0, base=0,
                               pattern=[[-1, 3]], channel_multiplier=1).then_inc(consts, 1)

            for s in range(LAST_STEP):
                if (n := s // G + 2) < N and s % G == 2 and SEQ[n][0] == 0 and n >= 2:
                    norm_scale(0, SEQ[n][1])
                if (b := batch_at(FIRST, s, BACK + 1)) is not None:
                    norm_scale(1, b)
                if (b := batch_at(SECOND, s, OUT_PROJECT + 1)) is not None:
                    norm_scale(2, b)
                    if b == 0:
                        pool.wait_ge(w_in, W_ALL)
                    h_of(b)
                if 0 <= s - 2 < JOBS and SEQ[(s - 2) // G][0] == 0:
                    window(s - 2, 0)
                    window(s - 2, 1)
                if (b := batch_at(FIRST, s, BACK + 2)) is not None:
                    if b == 0:
                        pool.wait_ge(w_in, W_ALL)
                    source_bias(b)
                for n in range(2, N):
                    if s == HIGH_STEP[n]:
                        keys_low(n)
                        queries_low(n)
                for n in range(1, N):
                    for gp in range(2):
                        if s == STEP_OF_STACK[(n, gp)] + (gp if STEP_OF_STACK[(n, 0)] == STEP_OF_STACK[(n, 1)] else 0):
                            blocks(n, gp)
                for b in range(B):
                    if s == FINISH_STEP[b]:
                        finish(b)

        @block.vector
        def _(dve):
            for k in range(3):
                dve.memset(values[k][:].rearrange("p t h c -> p (t h c)"), 0.0).then_inc(consts_v, 1)
            dve.wait_ge(consts_v, 3)
            for k in range(3):
                dve.memset(values[k][:, :, :, HD:HD + 1], 1.0).then_inc(consts_v, 1)

            def norm_stats(k, v, b):
                for t in range(TT):
                    dve.bn_stats(stats[k][:, t, :], v[:, t, :]).then_inc(bn[k], 1)
                dve.wait_ge(bn[k], (b + 1) * TT)
                for t in range(TT):
                    dve.bn_aggr(mean_var[k][:, t, :], stats[k][:, t, :]).then_inc(ag[k], 1)
                dve.wait_ge(ag[k], (b + 1) * TT)
                dve.tensor_scalar(var_eps[k][:], mean_var[k][:, :, 1], EPS, None, ALU.add).then_inc(ve[k], 1)

            def normalise(k, dst, v, b):
                dve.wait_ge(rs[k], b + 1)
                for t in range(TT):
                    dve.tensor_scalar(dst[:, t, :], v[:, t, :], mean_var[k][:, t, 0:1], rstd[k][:, t:t + 1],
                                      ALU.subtract, ALU.mult).then_inc(nm[k], 1)

            def norm1_stats(b):
                dve.wait_ge(x_in[b], 16)
                norm_stats(0, xb[b], b)

            def norm1(b):
                if b >= 2:
                    dve.wait_ge(q_tok_done, SEQ.index((0, b - 2)) + 1)
                normalise(0, xn[b % 2], xb[b], b)

            norm1_stats(0)
            norm1(0)
            norm1_stats(1)
            dve.memset(mx_hi[:].rearrange("p a b c -> p (a b c)"), 0.0).then_inc(consts_v, 1)
            norm1(1)
            dve.wait_ge(consts, 3)
            for k in range(3):
                dve.tensor_copy(keys_bd[k][GR:P, :, :, :].rearrange("p g h s -> p g (h s)")
                                .rearrange("p g (h s) -> p g h s", s=S),
                                head_rows[GR:P, :].rearrange("p (u h o) -> p u h o", u=1, o=1)
                                .to_broadcast([P - GR, G, HG, S])).then_inc(consts_v, 1)
                if k == 0:
                    dve.tensor_copy(ident_b[:], ident[:]).then_inc(ident_b_done, 1)
                    dve.memset(ones_bf[:], 1.0).then_inc(ident_b_done, 1)

            def sm_wait(use):
                dve.wait_ge(sm_full, SM_USE[use] + 1)
                return SM[SM_USE[use] % 2]

            def maximum(job, j):
                tile = sm_wait(("scores", job, j))
                dve.tensor_reduce(mx[:, job % 2, j // 2, 2 * (j % 2):2 * (j % 2) + 2],
                                  tile[:].rearrange("p (h k) -> p h k", k=S), AX.X, ALU.max)\
                    .then_inc(sm_done, 1)

            def minus_maxima(job):
                dve.wait_ge(sm_done, SM_USE[("scores", job, 3)] + 1)
                if job >= 2:
                    dve.wait_ge(mb_done, MB_USE[("maxima", job - 2)] + 1)
                pairs = mx_hi[:, job % 2, :, GR:GR + 2 * HG].rearrange("p t (h s) -> p t h s", s=2)
                dve.tensor_scalar(pairs[:, :, :, 0].bitcast(F32R), mx[:, job % 2], -1.0, None, ALU.mult)\
                    .then_inc(mxh_done, 1)
                dve.wait_ge(mxh_done, job + 1)
                dve.scalar_tensor_tensor(out=pairs[:, :, :, 1].bitcast(F32R), in0=mx[:, job % 2], scalar=-1.0,
                                         in1=pairs[:, :, :, 0], op0=ALU.mult, op1=ALU.subtract)\
                    .then_inc(mxl_done, 1)

            def divide(n, t):
                tile = sm_wait(("back", n, t))[:].rearrange("p (h c) -> p h c", c=VC)
                dve.reciprocal(recip[:, t, :], tile[:, :, HD]).then_inc(recip_done, 1)
                dve.wait_ge(recip_done, n * TT + t + 1)
                dve.tensor_tensor(att[:, t, :].rearrange("p (h e) -> p h e", e=HD), tile[:, :, 0:HD],
                                  recip[:, t, :].rearrange("p (h o) -> p h o", o=1)
                                  .to_broadcast([P, H, HD]), ALU.mult).then_inc(sm_done, 1)

            def first_residual(b):
                dve.wait_ge(sm_done, SM_USE[("back", SEQ.index((0, b)), 1)] + 1)
                dve.tensor_tensor(x1[b][:], xb[b][:], att[:], ALU.add).then_inc(x1_done, 1)
                dve.wait_ge(x1_done, b + 1)
                norm_stats(1, x1[b], b)

            def source(b):
                if b:
                    dve.wait_ge(srcbo_done, b)
                normalise(1, src, x1[b], b)

            def add_bias(b, t):
                if b == 0:
                    dve.wait_ge(w_in, W_ALL)
                else:
                    n = SEQ.index((1, b - 1))
                    dve.wait_ge(v_done, n + 1)
                    dve.wait_ge(q_tok_done, n + 1)
                tile = sm_wait(("project", b, t))
                dve.tensor_tensor(qkv[:, t, :], tile[:, 0:3 * D], bqkv[:], ALU.add).then_inc(sm_done, 1)

            def second_residual(b, t):
                dve.wait_ge(srcbo_done, b + 1)
                tile = sm_wait(("out_project", b, t))
                dve.tensor_tensor(res[:, t, :], tile[:, 0:D], src_bo[b][:, t, :], ALU.add).then_inc(sm_done, 1)

            def router(b):
                dve.wait_ge(h_done, b + 1)
                r = [0]

                def step(ins):
                    r[0] += 1
                    ins.then_inc(route, 1)
                    if r[0] < ROUTE:
                        dve.wait_ge(route, b * ROUTE + r[0])

                for t in range(TT):
                    step(dve.scalar_tensor_tensor(out=junk[:, t, :], in0=h[:, t, :], scalar=1.0, in1=rw_b[:],
                                                  op0=ALU.mult, op1=ALU.mult, accum_out=key[:, t:t + 1]))
                step(dve.tensor_scalar(key_b[:], key[:], rb_b[:, 0:1], None, ALU.add))
                step(dve.tensor_copy(key_i[:], key_b[:]))
                step(dve.tensor_copy(key_f[:], key_i[:]))
                step(dve.tensor_tensor(key_gt[:], key_f[:], key_b[:], ALU.is_gt))
                step(dve.tensor_tensor(key_fl[:], key_f[:], key_gt[:], ALU.subtract))
                step(dve.tensor_copy(key_fi[:], key_fl[:]))
                step(dve.tensor_scalar(expert[:], key_fi[:], NE - 1, None, ALU.bitwise_and))
                step(dve.tensor_copy(expert_f[:], expert[:]))
                for e in range(NE):
                    step(dve.tensor_scalar(chosen[:, b % 2, e, :], expert_f[:], float(e), None, ALU.is_equal))

            def add_expert(b, e):
                dve.wait_ge(down_done, b * 8 + 2 * (e + 1))
                if e == 0:
                    dve.wait_ge(route, (b + 1) * ROUTE)
                    if b:
                        dve.wait_ge(nm[3], b * TT)
                else:
                    dve.wait_ge(acc_done, b * 8 + 2 * e)
                base = h if e == 0 else acc
                for t in range(TT):
                    dve.scalar_tensor_tensor(out=acc[:, t, :], in0=Y[:, t * D:(t + 1) * D],
                                             scalar=chosen[:, b % 2, e, t:t + 1], in1=base[:, t, :],
                                             op0=ALU.mult, op1=ALU.add).then_inc(acc_done, 1)

            def setup_b2():
                r = [0]

                def step(ins):
                    r[0] += 1
                    ins.then_inc(b2_step, 1)
                    dve.wait_ge(b2_step, r[0])

                dve.wait_ge(wf_in, WF_ALL)
                dve.wait_ge(consts, 6)
                step(dve.tensor_copy(b2_part[:, 0, :], b2_3[:]))
                step(dve.tensor_tensor(b2_left[:, 0, :], b2_3[:], b2_part[:, 0, :], ALU.subtract))
                step(dve.tensor_copy(b2_part[:, 1, :], b2_left[:, 0, :]))
                step(dve.tensor_tensor(b2_left[:, 1, :], b2_left[:, 0, :], b2_part[:, 1, :], ALU.subtract))
                step(dve.tensor_copy(b2_part[:, 2, :], b2_left[:, 1, :]))
                step(dve.tensor_scalar(b2_pick[:, 0, :], b2_part[:, 0, :], b2_sel[:, 0:1], None, ALU.mult))
                step(dve.scalar_tensor_tensor(out=b2_pick[:, 1, :], in0=b2_part[:, 1, :],
                                              scalar=b2_sel[:, 1:2], in1=b2_pick[:, 0, :],
                                              op0=ALU.mult, op1=ALU.add))
                step(dve.scalar_tensor_tensor(out=b2_bf[:].rearrange("r e d -> r (e d)"),
                                              in0=b2_part[:, 2, :], scalar=b2_sel[:, 2:3],
                                              in1=b2_pick[:, 1, :], op0=ALU.mult, op1=ALU.add))

            for s in range(LAST_STEP):
                for slot in range(4):
                    if s < JOBS:
                        maximum(s, slot)
                    if slot == 3 and s < JOBS:
                        minus_maxima(s)
                    if slot >= 2:
                        n, g = divmod(s - BACK, G)
                        if g == 0 and 0 <= n < N:
                            divide(n, slot - 2)
                            if slot == 3 and SEQ[n][0] == 0:
                                first_residual(SEQ[n][1])
                    else:
                        if (b := batch_at(FIRST, s, PROJECT)) is not None:
                            add_bias(b, slot)
                        if (b := batch_at(SECOND, s, OUT_PROJECT)) is not None:
                            second_residual(b, slot)
                            if slot == 1:
                                dve.wait_ge(sm_done, SM_USE[("out_project", b, 1)] + 1)
                                norm_stats(2, res, b)
                    if slot == 0:
                        if (b := batch_at(FIRST, s, BACK + 1)) is not None:
                            source(b)
                        if (b := batch_at(SECOND, s, OUT_PROJECT + 1)) is not None:
                            normalise(2, res_n, res, b)
                        if (n := s // G + 2) < N and s % G == 1 and SEQ[n][0] == 0:
                            norm1_stats(SEQ[n][1])
                    if slot == 1 and (n := s // G + 2) < N and s % G == 2 and SEQ[n][0] == 0:
                        norm1(SEQ[n][1])
                    if slot == 3:
                        if (b := batch_at(SECOND, s, H_T)) is not None:
                            router(b)
                        if s == B1_STEP:
                            setup_b2()
                    for b, e in EXPERT_SUM_AT.get((s, slot), []):
                        add_expert(b, e)
                        if e == NE - 1:
                            dve.wait_ge(acc_done, b * 8 + 8)
                            norm_stats(3, acc, b)
                            normalise(3, acc_n, acc, b)

        @block.scalar
        def _(act):
            for b in range(2):
                act.dma_start(cb[b][:], cr[b]).then_inc(c_in[b], 16)

            def high_part(dst, v, slots, done):
                stack = dst[:].rearrange("p t (h s e) -> p t h s e", s=TERMS, e=HD)
                a, z = slots
                for t in range(TT):
                    ins = act.copy(stack[:, t, :, a:z + 1:z - a, :],
                                   by_head(v)[:, t].rearrange("p h (o e) -> p h o e", o=1)
                                   .to_broadcast([P, H, 2, HD]))
                ins.then_inc(done, 1)

            def high_parts(n):
                keys, queries, vals = operands(n)
                a, b = SEQ[n]
                if a == 0:
                    act.wait_ge(c_in[b], 16)
                else:
                    act.wait_ge(sm_done, SM_USE[("project", b, 1)] + 1)
                high_part(k_tok[n % 3], keys, (0, 2), k_hi_done)
                if a == 0:
                    act.wait_ge(nm[0], (b + 1) * TT)
                high_part(q_tok[n % 3], queries, (0, 1), q_hi_done)
                if n < 3:
                    act.wait_ge(consts_v, 3)
                else:
                    act.wait_ge(pv_done, G * (n - 2))
                act.copy(values[n % 3][:, :, :, 0:HD], by_head(vals)).then_inc(v_done, 1)

            def st_wait(use):
                act.wait_ge(st_full, ST_USE[use] + 1)
                return ST[ST_USE[use] % 2]

            def stacks(n, k):
                tile = st_wait(("stacks", n, k))
                dst = k_rows[n % 3][:, 2 * k:2 * k + 2, :] if k < 2 else \
                    q_rows[n % 3][0:GR, 2 * (k - 2):2 * (k - 2) + 2, :]
                act.copy(dst, tile[0:GR, :].rearrange("p (g s) -> p g s", s=S)).then_inc(st_done, 1)

            def small(dst, src_ap, use):
                act.wait_ge(mb_full, MB_USE[use] + 1)
                act.copy(dst, src_ap).then_inc(mb_done, 1)

            def exps(job, j):
                if j == 0 and job >= 2:
                    act.wait_ge(pv_done, job - 1)
                tile = st_wait(("scores", job, j))
                act.activation(probs[:, job % 2, j // 2, 2 * (j % 2):2 * (j % 2) + 2, :],
                               tile[:].rearrange("p (h q) -> p h q", q=S), ACT.Exp,
                               scale=SCALE2 if SEQ[job // G][0] else 1.0).then_inc(st_done, 1)

            def evacuate_heads(job):
                k = job % G // 2
                act.wait_ge(pv_done, job + 1)
                act.copy(heads_t[:, 2 * k:2 * k + 2, :], PO[:].rearrange("p (g s) -> p g s", s=S))\
                    .then_inc(po_done, 1)

            def relu(b, u):
                if u >= 2:
                    act.wait_ge(down_done, b * 8 + (u - 1))
                act.wait_ge(up_full, b * 8 + (u + 1))
                for c in range(2):
                    ins = act.activation(hid[:, u % 2, c, :], UP[:, c * S:(c + 1) * S], ACT.Relu,
                                         bias=b1_cols[:, 2 * u + c:2 * u + c + 1])
                ins.then_inc(up_done, 1)

            high_parts(0)
            for s in range(-1, LAST_STEP):
                if s == 0:
                    high_parts(1)
                if s - 4 >= 0 and (s - 4) % 2 == 1 and s - 4 < JOBS:
                    evacuate_heads(s - 4)
                for slot in range(4):
                    for n, k in STACKS_AT.get((s, slot), []):
                        stacks(n, k)
                    if slot == 0 and (b := batch_at(FIRST, s, SRC_T)) is not None:
                        small(src_t[:], MB[:, 0:S], ("src", b))
                    if slot == 0 and (b := batch_at(SECOND, s, H_T)) is not None:
                        small(h_t[b % 2][:], MB[:, 0:S], ("h", b))
                    if 0 <= s - 2 < JOBS:
                        exps(s - 2, slot)
                    if slot == 1 and 0 <= s - 1 < JOBS:
                        n, g = divmod(s - 1, G)
                        small(q_rows[n % 3][GR:P, g, :], MB[GR:P, 0:S], ("maxima", s - 1))
                    if slot == 2 and (b := batch_at(SECOND, s, ATT_T)) is not None:
                        small(att_t[:], MB[:, 0:S], ("att", b))
                    if slot == 2 and s == B1_STEP:
                        small(b1_cols[:], MB[:, 0:NE * FC], ("b1",))
                    for b, u in RELU_AT.get((s, slot), []):
                        relu(b, u)
                for n in range(2, N):
                    if s == HIGH_STEP[n]:
                        high_parts(n)

        @block.tensor
        def _(pe):
            def ring(done, n):
                if n >= 2:
                    pe.wait_ge(done, n - 1)

            def single(done, n):
                if n >= 1:
                    pe.wait_ge(done, n)

            def stacks(n, k):
                if k % 2 == 0:
                    pe.wait_ge(k_tok_done if k < 2 else q_tok_done, n + 1)
                tok = (k_tok if k < 2 else q_tok)[n % 3]
                use = ST_USE[("stacks", n, k)]
                ring(st_done, use)
                for g in range(2):
                    for t in range(TT):
                        c = (2 * (k % 2) + g) * GR
                        ins = pe.transpose(ST[use % 2][0:GR, g * S + t * P:g * S + (t + 1) * P],
                                           tok[:, t, c:c + GR].bitcast(F32), ident[:])
                ins.then_inc(st_full, 1)

            def query_major(job, j):
                n, g = divmod(job, G)
                qt, pr = divmod(j, 2)
                if j == 0:
                    pe.wait_ge(st_done, ST_USE[("stacks", n, 2 + g // 2)] + 1)
                if qt == 0:
                    pe.wait_ge(kbd_done, 8 * n + 4 * (g // 2) + 2 * pr + 2)
                use = SM_USE[("scores", job, j)]
                ring(sm_done, use)
                ins = pe.matmul(SM[use % 2][:], q_rows[n % 3][0:GR, g, qt * P:(qt + 1) * P],
                                keys_bd[n % 3][0:GR, g, 2 * pr:2 * pr + 2, :], start=True, stop=True)
                if SEQ[n][0] == 0:
                    kt = 1 - qt
                    tri = SM[use % 2][:].rearrange("p (h k) -> p h k", k=S)[:, :, kt * P:(kt + 1) * P]
                    ins = pe.matmul(tri, ident_b[:], (mask_above, mask_below)[qt][:],
                                    start=False, stop=True, skip_group_check=True)
                ins.then_inc(sm_full, 1)

            def turn_maxima(job):
                pe.wait_ge(mxl_done, job + 1)
                single(mb_done, MB_USE[("maxima", job)])
                for qt in range(TT):
                    ins = pe.transpose(MB[:, qt * P:(qt + 1) * P], mx_hi[:, job % 2, qt, :], ident[:])
                ins.then_inc(mb_full, 1)

            def key_major(job, j):
                n, g = divmod(job, G)
                kb, pr = divmod(j, 2)
                if j == 0:
                    pe.wait_ge(mb_done, MB_USE[("maxima", job)] + 1)
                use = ST_USE[("scores", job, j)]
                ring(st_done, use)
                for i in range(2):
                    ins = pe.matmul(ST[use % 2][:, i * S:(i + 1) * S],
                                    keys_bd[n % 3][:, g, 2 * pr + i, kb * P:(kb + 1) * P],
                                    q_rows[n % 3][:, g, :], start=True, stop=True)
                ins.then_inc(st_full, 1)

            def weigh(job, kb):
                n, g = divmod(job, G)
                if SEQ[n][0] == 0:
                    pe.wait_ge(tri_done, 2 * (FIRST_JOBS.index(job)) + kb + 1)
                pe.wait_ge(st_done, ST_USE[("scores", job, 2 * kb + 1)] + 1)
                if g == 0 and kb == 0:
                    pe.wait_ge(v_done, n + 1)
                if g % 2 == 0 and kb == 0:
                    single(po_done, job // 2)
                for hh in range(HG):
                    ins = pe.matmul(PO[VC * hh:VC * (hh + 1), (g % 2) * S:(g % 2 + 1) * S],
                                    values[n % 3][:, kb, HG * g + hh, :], probs[:, job % 2, kb, hh, :],
                                    start=(kb == 0), stop=(kb == TT - 1))
                if kb == TT - 1:
                    ins.then_inc(pv_done, 1)

            def back(n, t):
                pe.wait_ge(po_done, 2 * n + 2)
                use = SM_USE[("back", n, t)]
                ring(sm_done, use)
                for g in range(G):
                    ins = pe.transpose(SM[use % 2][:, g * P:(g + 1) * P], heads_t[:, g, t * P:(t + 1) * P],
                                       ident[:])
                ins.then_inc(sm_full, 1)

            def turn_small(v, use):
                single(mb_done, MB_USE[use])
                for t in range(TT):
                    ins = pe.transpose(MB[:, t * P:(t + 1) * P], v[:, t, :], ident[:])
                ins.then_inc(mb_full, 1)

            def project(lhs, rhs, width, t, of, use):
                pe.wait_ge(mb_done, MB_USE[of] + 1)
                n = SM_USE[use]
                ring(sm_done, n)
                pe.matmul(SM[n % 2][:, 0:width], lhs[:, t * P:(t + 1) * P], rhs[:], start=True, stop=True)\
                    .then_inc(sm_full, 1)

            def up(b, u):
                if u == 0:
                    pe.wait_ge(mb_done, MB_USE[("h", b)] + 1)
                single(up_done, b * 8 + u)
                e = u // 2
                for c in range(2):
                    f = (2 * (u % 2) + c) * P
                    ins = pe.matmul(UP[:, c * S:(c + 1) * S], w1[:, e, f:f + P], h_t[b % 2][:], start=True, stop=True)
                ins.then_inc(up_full, 1)

            def down(b, u):
                e = u // 2
                if u % 2 == 0:
                    single(acc_done, b * 8 + 2 * e)
                    pe.matmul(Y[:, 0:TT * D], ones_bf[:],
                              b2_bf[:, e, :].rearrange("r (o d) -> r o d", o=1).to_broadcast([TERMS, TT, D]),
                              start=True, stop=False, skip_group_check=True)
                pe.wait_ge(up_done, b * 8 + (u + 1))
                for c in range(2):
                    for t in range(TT):
                        ins = pe.matmul(Y[:, t * D:(t + 1) * D], hid[:, u % 2, c, t * P:(t + 1) * P],
                                        w2[:, e, 2 * (u % 2) + c, :], start=False,
                                        stop=(u % 2 == 1 and c == 1), skip_group_check=True)
                ins.then_inc(down_done, 1)

            pe.wait_ge(consts, 1)
            for s in range(-1, LAST_STEP):
                if s == 0:
                    pe.wait_ge(consts, 5)
                    pe.wait_ge(ident_b_done, 2)
                    pe.wait_ge(consts_v, 8)
                if s == 2:
                    pe.wait_ge(consts_v, CONST_V)
                for slot in range(4):
                    if 0 <= s < JOBS:
                        query_major(s, slot)
                    if slot >= 2:
                        n, g = divmod(s - BACK, G)
                        if g == 0 and 0 <= n < N:
                            back(n, slot - 2)
                    else:
                        if (b := batch_at(FIRST, s, PROJECT)) is not None:
                            if b == 0:
                                pe.wait_ge(w_in, W_ALL)
                            project(src_t, wqkv, 3 * D, slot, ("src", b), ("project", b, slot))
                        if (b := batch_at(SECOND, s, OUT_PROJECT)) is not None:
                            project(att_t, wo, D, slot, ("att", b), ("out_project", b, slot))
                    for n, k in STACKS_AT.get((s, slot), []):
                        stacks(n, k)
                    if slot == 0 and (b := batch_at(FIRST, s, SRC_T)) is not None:
                        pe.wait_ge(nm[1], (b + 1) * TT)
                        turn_small(src, ("src", b))
                    if slot == 0 and (b := batch_at(SECOND, s, H_T)) is not None:
                        pe.wait_ge(h_done, b + 1)
                        turn_small(h, ("h", b))
                    if 0 <= s - 2 < JOBS:
                        key_major(s - 2, slot)
                    if slot == 1 and 0 <= s - 1 < JOBS:
                        turn_maxima(s - 1)
                    if slot == 2 and (b := batch_at(SECOND, s, ATT_T)) is not None:
                        pe.wait_ge(sm_done, SM_USE[("back", SEQ.index((1, b)), 1)] + 1)
                        turn_small(att, ("att", b))
                    if slot == 2 and s == B1_STEP:
                        pe.wait_ge(wf_in, WF_ALL)
                        single(mb_done, MB_USE[("b1",)])
                        pe.transpose(MB[:, 0:NE * FC], b1_rows[:], ident[0:NE * FC, 0:NE * FC])\
                            .then_inc(mb_full, 1)
                    if slot % 2 == 1 and 0 <= s - 3 < JOBS:
                        weigh(s - 3, slot // 2)
                    for b, q in EXPERTS_AT.get((s, slot), []):
                        if q > 0:
                            if q == 1 and b == 0:
                                pe.wait_ge(b2_step, 8)
                            down(b, q - 1)
                        if q < 8:
                            up(b, q)


_INS = ["x", "ctx_1024"] + ["L0_ffn_" + n for n in (
    "Wq", "bq", "Wk", "bk", "Wv", "bv", "Wo", "bo", "router_w", "router_b", "W1", "b1", "W2", "b2",
    "ln1_g", "ln1_b", "ln2_g", "ln2_b")]


def kernel(**inputs):
    import concourse.bacc as bacc
    from concourse.bass_utils import run_bass_kernel_spmd

    nc = bacc.Bacc("TRN2", target_bir_lowering=False, num_devices=1)
    arrays, args = {}, []
    for name in _INS:
        a = np.ascontiguousarray(inputs[name])
        arrays[f"in_{name}"] = a
        args.append(nc.dram_tensor(f"in_{name}", a.shape, mybir.dt.from_np(a.dtype), kind="ExternalInput").ap())
    args.append(nc.dram_tensor("out_0", (B, S, D), F32, kind="ExternalOutput").ap())
    build(nc, *args)
    r = run_bass_kernel_spmd(nc, [arrays], core_ids=[0])
    return r.results[0]["out_0"]
```

```python
from contextlib import ExitStack

import numpy as np
import concourse.bass as bass
from concourse import mybir

ALU = mybir.AluOpType
ACT = mybir.ActivationFunctionType
AX = mybir.AxisListType
F32 = mybir.dt.float32
F32R = mybir.dt.float32r
BF16 = mybir.dt.bfloat16
I32 = mybir.dt.int32

P = 128
B, S = 4, 256
TT = S // P
D = 128
H = 16
HD = D // H
G = 4
HG = H // G
TERMS = 3
HR = TERMS * HD
GR = HG * HR
VC = 32
NE = 4
FF = 512
FC = FF // P
EPS = 1e-5
MASKED = -1.0e30
SCALE2 = float(HD) ** -0.5

SEQ = [(0, 0), (0, 1), (0, 2), (1, 0), (0, 3), (1, 1), (1, 2), (1, 3)]
N = len(SEQ)
JOBS = G * N
FIRST = [G * SEQ.index((0, b)) for b in range(B)]
SECOND = [G * SEQ.index((1, b)) for b in range(B)]

TURN_SLOT = 2


def plan():
    when = {}

    def due(piece, step, slot, *which):
        when.setdefault(piece, {}).setdefault((step + slot // 4, slot % 4), []).append(which)

    for n, (a, b) in enumerate(SEQ):
        start = G * n
        tight = a == 1 and start - FIRST[b] == 3 * G
        if n >= 2:
            high = (FIRST[b] + 10, -1) if a else (start - 5, 1)
            due("keys_high", *high, n)
            due("queries_high", high[0], high[1] + 2, n)
            due("place_values", 0, max(4 * high[0] + high[1] + 2, 4 * (G * (n - 2) + 3)), n)
            due("keys_low", high[0], high[1] + 2, n)
            due("queries_low", high[0], high[1] + 3, n)
        if n == 0:
            turned = (-4, -3, -2, -1)
        elif n == 1:
            turned = (-12, -9, -8, -4)
        elif tight:
            turned = (-4, -3, -2, 0)
        else:
            turned = (-12, -11, -8, -4)
        for k, slot in enumerate(turned):
            due("stacks", start, slot, n, k)
        if n:
            for gp in range(2):
                due("blocks", start, (-3, -1)[gp] if tight else (-8, -3)[gp], n, gp)
        for t in range(TT):
            due("back", start + 7, 2 + t, n, t)

    for b in range(B):
        f, g = FIRST[b], SECOND[b]
        if b >= 2:
            due("norm1_stats", f - 7, 0, b)
            due("scale", f - 7, 4, 0, b)
            due("norm1", f - 6, 2, b)
        due("scale", f + 8, 0, 1, b)
        due("source", f + 8, 1, b)
        due("source_bias", f + 9, -1, b)
        due("src_t", f + 8, 4, b)
        for t in range(TT):
            due("project", f + 9, 1 + t, b, t)
            due("out_project", g + 8, 3 + t, b, t)
        due("att_t", g + 8, 1, b)
        due("scale", g + 9, 1, 2, b)
        due("h", g + 9, 2, b)
        due("h_t", g + 10, 1, b)
        due("router", g + 9, 4, b)
        for q in range(2 * NE + 1):
            step, slot = {
                0: (23, 4 * q),
                1: (31, 2 * q),
                2: (35, 2 * q),
                3: (39, -1 + 3 * q),
            }[b]
            due("experts", step, slot, b, q)
            if q and q % 2 == 0:
                due("expert_sum", step, slot + 1, b, q // 2 - 1)
                if q == 2 * NE:
                    due("scale", step, slot + 1, 3, b)
    due("b1", 14, 0)
    for part in range(2):
        due("b2", 14, part - 1, part)
    for g in range(G):
        due("max_rows", 0, 2 - g, 1, g)
        due("max_rows", 4, 5 + 4 * g, 2, g)
    for e in range(NE):
        due("w1_high", 16, 4 * e, e)
        due("w1_low", 16, 4 * e + 1, e)
    return when


PLAN = plan()
LAST_STEP = 1 + max(step for spots in PLAN.values() for step, _ in spots)


def due(piece, step, slot):
    return PLAN[piece].get((step, slot), [])


def number(uses):
    return {use: k for k, use in enumerate(uses)}


def act_uses():
    for s in range(-1, LAST_STEP):
        for slot in range(4):
            for piece in ("stacks", "src_t", "att_t", "h_t", "b1"):
                yield from ((piece, *which) for which in due(piece, s, slot))
            if 0 <= s - 2 < JOBS:
                yield ("scores", s - 2, slot)
            if slot == TURN_SLOT and 0 <= s - 1 < JOBS:
                yield ("maxima", s - 1)
            yield from (("up", b, q) for b, q in due("experts", s, slot) if q < 2 * NE)


def dve_uses():
    for s in range(LAST_STEP):
        for slot in range(4):
            if s < JOBS:
                yield ("scores", s, slot)
            for piece in ("back", "project", "out_project"):
                yield from ((piece, *which) for which in due(piece, s, slot))


FIRST_JOBS = [j for j in range(JOBS) if SEQ[j // G][0] == 0]
ACT_USE, DVE_USE = number(act_uses()), number(dve_uses())
ACT_BANKS = DVE_BANKS = 3
FIRST_EXPERT = min(step for step, _ in PLAN["experts"])


def dve_places():
    places, last, n = {}, {}, 0
    for use, k in DVE_USE.items():
        early = k < DVE_USE[("scores", FIRST_EXPERT, 0)]
        bank = k % (DVE_BANKS + 1) if early else n % DVE_BANKS
        n += not early
        places[use] = bank, last.get(bank, -1) + 1
        last[bank] = k
    return places


DVE_PLACE = dve_places()


def build(nc, x, ctx_in, Wq, bq, Wk, bk, Wv, bv, Wo, bo, rw, rb, W1, b1, W2, b2, g1, be1, g2, be2, out):
    with ExitStack() as ctx:
        def sb(name, shape, dt=F32):
            return ctx.enter_context(nc.sbuf_tensor(name, shape, dt))

        def bank(name):
            return ctx.enter_context(nc.psum_tensor(name, [P, 512], F32))

        def sem(name):
            return ctx.enter_context(nc.semaphore(name))

        xb = [sb(f"xb{b}", [P, TT, D]) for b in range(B)]
        cb = [sb(f"cb{b}", [P, TT, D]) for b in range(B)]
        wqkv = sb("wqkv", [P, 3 * D])
        bqkv = sb("bqkv", [P, 3 * D])
        wo = sb("wo", [P, D])
        bo_b = sb("bo_b", [P, D])
        rw_b = sb("rw_b", [P, D])
        rb_b = sb("rb_b", [P, 1])
        g1_b = sb("g1_b", [P, D])
        be1_b = sb("be1_b", [P, D])
        g2_b = sb("g2_b", [P, D])
        be2_b = sb("be2_b", [P, D])
        w1 = sb("w1", [P, NE, FF])
        w2 = sb("w2", [P, NE, FC, D])
        b1_rows = sb("b1_rows", [NE * FC, P])
        b1_cols = sb("b1_cols", [P, NE * FC])
        b2_twice = sb("b2_twice", [2, NE * D])
        ident = sb("ident", [P, P])
        ident_b = sb("ident_b", [P, P], BF16)
        ident_r = sb("ident_r", [P, P], F32R)
        mask_above = sb("mask_above", [P, 2, P], BF16)
        mask_below = sb("mask_below", [P, 2, P], BF16)
        head_rows = sb("head_rows", [P, HG])
        half = sb("half", [P, TT])
        b2_high = sb("b2_high", [2, NE * D], F32R)
        b2_second = sb("b2_second", [2, 1])
        b2_rows = sb("b2_rows", [2, NE, D], F32R)
        ones_2 = sb("ones_2", [2, P])
        ones_r = sb("ones_r", [2, P], F32R)
        w1_high = sb("w1_high", [P, NE, FF], F32R)
        w1_low = sb("w1_low", [P, NE, FF], F32R)
        stats = [sb(f"stats{k}", [P, TT, 6]) for k in range(4)]
        mean_var = [sb(f"mean_var{k}", [P, TT, 2]) for k in range(4)]
        var_eps = [sb(f"var_eps{k}", [P, TT]) for k in range(4)]
        rstd = [sb(f"rstd{k}", [P, TT]) for k in range(4)]
        xn = [sb(f"xn{k}", [P, TT, D]) for k in range(2)]
        q_tok = [sb(f"q_tok{a}", [P, TT, H * HR], F32R) for a in range(2)]
        k_tok = [sb(f"k_tok{a}", [P, TT, H * HR], F32R) for a in range(2)]
        q_rows = [sb(f"q_rows{a}", [P, G, S], F32R) for a in range(3)]
        k_rows = [sb(f"k_rows{a}", [GR, G, S]) for a in range(3)]
        keys_bd = [sb(f"keys_blockdiag{a}", [P, G, HG, S], F32R) for a in range(3)]
        values = [sb(f"values{a}", [P, TT, H, VC]) for a in range(3)]
        maxima = sb("maxima", [P, 2, TT, HG])
        minus_maxima_cols = sb("minus_maxima_cols", [P, 2, TT, P])
        probs = sb("probs", [P, 2, TT, HG, S])
        heads_t = sb("heads_t", [P, G, S])
        recip = sb("recip", [P, TT, H])
        att = sb("att", [P, TT, D])
        x1 = [sb(f"x1_{b}", [P, TT, D]) for b in range(B)]
        src = sb("src", [P, TT, D])
        src_bo = [sb(f"src_bo{b}", [P, TT, D]) for b in range(B)]
        src_t = sb("src_t", [P, S])
        qkv = sb("qkv", [P, TT, 3 * D])
        att_t = sb("att_t", [P, S])
        res = sb("res", [P, TT, D])
        res_g = sb("res_g", [P, TT, D])
        h = sb("h", [P, TT, D])
        h_t = sb("h_t", [P, S])
        h_high_t = [sb(f"h_high_t{k}", [P, S], F32R) for k in range(2)]
        h_low_t = [sb(f"h_low_t{k}", [P, S], F32R) for k in range(2)]
        junk = sb("junk", [P, D])
        key = sb("key", [P, TT])
        key_b = sb("key_b", [P, TT])
        key_i = sb("key_i", [P, TT], I32)
        key_gt = sb("key_gt", [P, TT])
        key_fi = sb("key_fi", [P, TT], I32)
        expert = sb("expert", [P, TT], I32)
        chosen = sb("chosen", [P, 2, NE, TT])
        hid = sb("hid", [P, 2, 2, S])
        acc = sb("acc", [P, TT, D])
        acc_g = sb("acc_g", [P, TT, D])
        x1_b2 = xb
        act_banks = [bank(f"act_bank{k}") for k in range(ACT_BANKS)]
        dve_banks = [bank(f"dve_bank{k}") for k in range(DVE_BANKS)]
        HEADS = bank("HEADS")
        Y = bank("Y")
        dve_banks.append(Y)
        x_in = [sem(f"x_in{b}") for b in range(B)]
        c_in = [sem(f"c_in{b}") for b in range(B)]
        weights_in, expert_weights_in = sem("weights_in"), sem("expert_weights_in")
        consts = sem("consts")
        dve_consts = sem("dve_consts")
        values_clear = sem("values_clear")
        dve_idents = sem("dve_idents")
        zeroed = sem("zeroed")
        sel_done = sem("sel_done")
        b2_step = sem("b2_step")
        act_bank_full, act_bank_read = sem("act_bank_full"), sem("act_bank_read")
        dve_bank_full, dve_bank_read = sem("dve_bank_full"), sem("dve_bank_read")
        heads_read = sem("heads_read")
        weighed = sem("weighed")
        down_done = sem("down_done")
        stats_done = [sem(f"stats_done_{k}") for k in range(4)]
        mean_var_done = [sem(f"mean_var_done_{k}") for k in range(4)]
        var_eps_done = [sem(f"var_eps_done_{k}") for k in range(4)]
        rstd_done = [sem(f"rstd_done_{k}") for k in range(4)]
        norm_done = [sem(f"norm_done_{k}") for k in range(2)]
        keys_high_done, queries_high_done = sem("keys_high_done"), sem("queries_high_done")
        queries_low_done, keys_low_done = sem("queries_low_done"), sem("keys_low_done")
        values_done = sem("values_done")
        blocks_done = sem("blocks_done")
        first_blocks_done = sem("first_blocks_done")
        maxima_high_done = sem("maxima_high_done")
        maxima_low_done = sem("maxima_low_done")
        window_done = sem("window_done")
        recip_done = sem("recip_done")
        x1_done = sem("x1_done")
        src_bo_done = sem("src_bo_done")
        h_done, h_low_done = sem("h_done"), sem("h_low_done")
        w1_high_done, w1_low_done = sem("w1_high_done"), sem("w1_low_done")
        max_rows_done = sem("max_rows_done")
        gain_done = [sem(f"gain_done{k}") for k in range(4)]
        route = sem("route")
        acc_done = sem("acc_done")
        x1_b2_done = sem("x1_b2_done")
        out_done, stored = sem("out_done"), sem("stored")

        block = ctx.enter_context(nc.Block())

        xr = x.rearrange("b (t p) d -> b p t d", p=P)
        cr = ctx_in.rearrange("b (t p) d -> b p t d", p=P)
        outr = out.rearrange("b (t p) d -> b p t d", p=P)
        WEIGHTS_IN, EXPERT_WEIGHTS_IN = 16 * 14, 16 * 4
        DVE_CONSTS = 1 + G // 2
        ROUTER_STEPS = TT + 5 + NE

        def row(v):
            return v.rearrange("(a d) -> a d", a=1).to_broadcast([P, D])

        def by_head(v):
            return v.rearrange("p t (h e) -> p t h e", e=HD)

        def wide(v):
            return v[:].rearrange("p (o d) -> p o d", o=1).to_broadcast([P, TT, D])

        def expert_bank(b, e):
            return HEADS if b >= 2 and e % 2 else Y

        def operands(n):
            a, b = SEQ[n]
            if a == 0:
                return cb[b][:], xn[b % 2][:], cb[b][:]
            return qkv[:, :, D:2 * D], qkv[:, :, 0:D], qkv[:, :, 2 * D:3 * D]

        @block.sync
        def _(sp):
            for b in range(2):
                sp.dma_start(cb[b][:], cr[b]).then_inc(c_in[b], 16)
            for k, w in enumerate((Wq, Wk, Wv)):
                sp.dma_start(wqkv[:, k * D:(k + 1) * D], w).then_inc(weights_in, 16)
            for k, v in enumerate((bq, bk, bv)):
                sp.dma_start(bqkv[:, k * D:(k + 1) * D], row(v)).then_inc(weights_in, 16)
            sp.dma_start(wo[:], Wo).then_inc(weights_in, 16)
            for t, v in ((bo_b, bo), (g1_b, g1), (be1_b, be1), (g2_b, g2), (be2_b, be2)):
                sp.dma_start(t[:], row(v)).then_inc(weights_in, 16)
            sp.dma_start(rw_b[:], row(rw.rearrange("d a -> (d a)"))).then_inc(weights_in, 16)
            sp.dma_start(rb_b[:], rb.rearrange("(a d) -> a d", a=1).to_broadcast([P, 1])).then_inc(weights_in, 16)
            for b in range(2, B):
                sp.dma_start(cb[b][:], cr[b]).then_inc(c_in[b], 16)
                sp.dma_start(xb[b][:], xr[b]).then_inc(x_in[b], 16)
            sp.dma_start(b1_rows[:], b1.rearrange("e (c p) -> (e c) p", p=P)).then_inc(expert_weights_in, 16)
            sp.dma_start(b2_twice[:], b2.rearrange("e d -> (e d)").rearrange("(a n) -> a n", a=1)
                         .to_broadcast([2, NE * D])).then_inc(expert_weights_in, 16)
            sp.dma_start(w1[:], W1.rearrange("e d f -> d e f")).then_inc(expert_weights_in, 16)
            sp.dma_start(w2[:], W2.rearrange("e (c p) d -> p e c d", p=P)).then_inc(expert_weights_in, 16)
            for b in range(B):
                sp.wait_ge(out_done, (b + 1) * TT)
                sp.dma_start(outr[b], x1[b][:]).then_inc(stored, 16)
            sp.wait_ge(stored, 16 * B)

        @block.gpsimd
        def _(pool):
            pool.memset(ident[:], 0.0).then_inc(zeroed, 1)
            pool.memset(head_rows[:], 1.0).then_inc(zeroed, 1)
            pool.memset(half[:], -0.5).then_inc(zeroed, 1)
            pool.memset(ones_2[:], 1.0).then_inc(zeroed, 1)
            pool.wait_ge(zeroed, 4)
            pool.affine_select(out=ident[:], in_=ident[:], compare_op=ALU.not_equal, fill=1.0, base=0,
                               pattern=[[-1, P]], channel_multiplier=1).then_inc(consts, 1)

            def norm_scale(k, b):
                pool.wait_ge(var_eps_done[k], b + 1)
                pool.tensor_tensor(rstd[k][:], var_eps[k][:], half[:], ALU.pow).then_inc(rstd_done[k], 1)

            def low_part(dst, v, lo_slot, hi_slot, done):
                stack = dst[:].rearrange("p t (h s e) -> p t h s e", s=TERMS, e=HD)
                pool.tensor_tensor(stack[:, :, :, lo_slot, :], by_head(v),
                                   stack[:, :, :, hi_slot, :].bitcast(F32), ALU.subtract).then_inc(done, 1)

            def keys_low(n):
                pool.wait_ge(keys_high_done, n + 1)
                low_part(k_tok[n % 2], operands(n)[0], 1, 0, keys_low_done)

            def queries_low(n):
                pool.wait_ge(queries_high_done, n + 1)
                low_part(q_tok[n % 2], operands(n)[1], 2, 0, queries_low_done)

            def blocks(n, gp):
                pool.wait_ge(act_bank_read, ACT_USE[("stacks", n, gp)] + 1)
                for hh in range(HG):
                    pool.tensor_scalar(keys_bd[n % 3][0:GR, 2 * gp:2 * gp + 2, hh, :],
                                       k_rows[n % 3][:, 2 * gp:2 * gp + 2, :],
                                       head_rows[0:GR, hh:hh + 1], 0.0, ALU.mult, ALU.add)\
                        .then_inc(blocks_done, 1)

            def window(job, kb):
                pool.wait_ge(act_bank_read, ACT_USE[("scores", job, 2 * kb + 1)] + 1)
                sign = 1 if kb == 0 else -1
                p = probs[:, job % 2, kb, :, P:2 * P] if kb == 0 else probs[:, job % 2, kb, :, 0:P]
                pool.affine_select(out=p, in_=p, compare_op=ALU.is_ge, fill=0.0, base=0,
                                   pattern=[[0, HG], [-sign, P]], channel_multiplier=sign).then_inc(window_done, 1)

            def source_bias(b):
                pool.wait_ge(norm_done[1], (b + 1) * TT)
                pool.tensor_tensor(src_bo[b][:], src[:], wide(bo_b), ALU.add).then_inc(src_bo_done, 1)
                pool.tensor_tensor(x1_b2[b][:], x1[b][:], wide(be2_b), ALU.add).then_inc(x1_b2_done, 1)

            pool.memset(mask_above[:], 0.0).then_inc(zeroed, 1)
            pool.memset(mask_below[:], 0.0).then_inc(zeroed, 1)
            pool.memset(b2_second[:], -1.0).then_inc(zeroed, 1)
            pool.wait_ge(zeroed, 7)
            pool.affine_select(out=mask_above[:], in_=mask_above[:], compare_op=ALU.is_ge, fill=MASKED,
                               base=0, pattern=[[0, 2], [-1, P]], channel_multiplier=1).then_inc(consts, 1)
            pool.affine_select(out=mask_below[:], in_=mask_below[:], compare_op=ALU.is_ge, fill=MASKED,
                               base=0, pattern=[[0, 2], [1, P]], channel_multiplier=-1).then_inc(consts, 1)
            pool.affine_select(out=b2_second[:], in_=b2_second[:], compare_op=ALU.not_equal, fill=0.0, base=0,
                               pattern=[[0, 1]], channel_multiplier=1).then_inc(consts, 1)
            edges = ((0, GR, HR), (GR, P, 2))
            pool.wait_ge(consts, 4)
            for k, (lo, hi, n) in enumerate(edges):
                rows = head_rows[lo:hi, :]
                pool.affine_select(out=rows, in_=rows, compare_op=ALU.is_ge, fill=0.0, base=0,
                                   pattern=[[-n, HG]], channel_multiplier=1).then_inc(sel_done, 1)
                pool.wait_ge(sel_done, k + 1)
                pool.affine_select(out=rows, in_=rows, compare_op=ALU.is_ge, fill=0.0, base=n - 1,
                                   pattern=[[n, HG]], channel_multiplier=-1).then_inc(consts, 1)
                pool.wait_ge(consts, k + 5)
            keys_low(0)
            norm_scale(0, 0)
            keys_low(1)
            queries_low(0)
            norm_scale(0, 1)
            blocks(0, 1)
            queries_low(1)

            for s in range(LAST_STEP):
                for slot in range(4):
                    for k, b in due("scale", s, slot):
                        norm_scale(k, b)
                    for n, in due("keys_low", s, slot):
                        keys_low(n)
                    for n, in due("queries_low", s, slot):
                        queries_low(n)
                    for n, gp in due("blocks", s, slot):
                        blocks(n, gp)
                    if slot % 2 == 1 and 0 <= s - 2 < JOBS and SEQ[(s - 2) // G][0] == 0:
                        window(s - 2, slot // 2)
                    for e, in due("w1_low", s, slot):
                        pool.wait_ge(w1_high_done, e + 1)
                        pool.tensor_tensor(w1_low[:, e, :], w1[:, e, :], w1_high[:, e, :].bitcast(F32),
                                           ALU.subtract).then_inc(w1_low_done, 1)
                    for b, in due("source_bias", s, slot):
                        if b == 0:
                            pool.wait_ge(weights_in, WEIGHTS_IN)
                        source_bias(b)

        @block.vector
        def _(dve):
            def clear_values(k):
                dve.memset(values[k][:].rearrange("p t h c -> p (t h c)"), 0.0).then_inc(values_clear, 1)
                dve.wait_ge(values_clear, 2 * k + 1)
                dve.memset(values[k][:, :, :, HD:HD + 1], 1.0).then_inc(values_clear, 1)

            def norm_stats(k, v, b):
                for t in range(TT):
                    dve.bn_stats(stats[k][:, t, :], v[:, t, :]).then_inc(stats_done[k], 1)
                dve.wait_ge(stats_done[k], (b + 1) * TT)
                for t in range(TT):
                    dve.bn_aggr(mean_var[k][:, t, :], stats[k][:, t, :]).then_inc(mean_var_done[k], 1)
                dve.wait_ge(mean_var_done[k], (b + 1) * TT)
                dve.tensor_scalar(var_eps[k][:], mean_var[k][:, :, 1], EPS, None, ALU.add)\
                    .then_inc(var_eps_done[k], 1)

            def normalise(k, dst, v, b):
                dve.wait_ge(rstd_done[k], b + 1)
                for t in range(TT):
                    dve.tensor_scalar(dst[:, t, :], v[:, t, :], mean_var[k][:, t, 0:1], rstd[k][:, t:t + 1],
                                      ALU.subtract, ALU.mult).then_inc(norm_done[k], 1)

            def gained(k, dst, v, gain):
                for t in range(TT):
                    dve.scalar_tensor_tensor(out=dst[:, t, :], in0=v[:, t, :], scalar=mean_var[k][:, t, 0:1],
                                             in1=gain[:], op0=ALU.subtract, op1=ALU.mult)\
                        .then_inc(gain_done[k], 1)

            def scaled(k, dst, v, shift, b, done):
                dve.wait_ge(gain_done[k], (b + 1) * TT)
                dve.wait_ge(rstd_done[k], b + 1)
                for t in range(TT):
                    dve.scalar_tensor_tensor(out=dst[:, t, :], in0=v[:, t, :], scalar=rstd[k][:, t:t + 1],
                                             in1=shift[t], op0=ALU.mult, op1=ALU.add).then_inc(done, 1)

            def norm1_stats(b):
                dve.wait_ge(x_in[b], 16)
                norm_stats(0, xb[b], b)

            def norm1(b):
                if b >= 2:
                    dve.wait_ge(queries_low_done, SEQ.index((0, b - 2)) + 1)
                normalise(0, xn[b % 2], xb[b], b)

            dve.memset(minus_maxima_cols[:].rearrange("p a b c -> p (a b c)"), 0.0).then_inc(dve_consts, 1)
            dve.wait_ge(consts, 1)
            dve.tensor_copy(ident_r[:], ident[:]).then_inc(dve_idents, 1)
            dve.tensor_copy(ident_b[:], ident[:]).then_inc(dve_idents, 1)
            dve.tensor_copy(ones_r[:], ones_2[:]).then_inc(dve_idents, 1)
            clear_values(0)
            norm1_stats(0)
            clear_values(1)
            norm1(0)
            norm1_stats(1)

            def first_max_rows(g):
                dve.tensor_copy(keys_bd[0][GR:P, g, :, :],
                                head_rows[GR:P, :].rearrange("p (h o) -> p h o", o=1)
                                .to_broadcast([P - GR, HG, S])).then_inc(dve_consts, 1)

            dve.wait_ge(consts, 6)
            for g in range(G // 2):
                first_max_rows(g)
            dve.wait_ge(act_bank_read, ACT_USE[("stacks", 0, 0)] + 1)
            for hh in range(HG):
                dve.tensor_scalar(keys_bd[0][0:GR, 0:2, hh, :], k_rows[0][:, 0:2, :],
                                  head_rows[0:GR, hh:hh + 1], None, ALU.mult).then_inc(first_blocks_done, 1)
            norm1(1)

            def filled(use):
                dve.wait_ge(dve_bank_full, DVE_USE[use] + 1)
                return dve_banks[DVE_PLACE[use][0]]

            def maximum(job, j):
                tile = filled(("scores", job, j))
                dve.tensor_reduce(maxima[:, job % 2, j // 2, 2 * (j % 2):2 * (j % 2) + 2],
                                  tile[:].rearrange("p (h k) -> p h k", k=S), AX.X, ALU.max)\
                    .then_inc(dve_bank_read, 1)

            def minus_maxima(job):
                dve.wait_ge(dve_bank_read, DVE_USE[("scores", job, 3)] + 1)
                if job >= 2:
                    dve.wait_ge(act_bank_full, ACT_USE[("maxima", job - 2)] + 1)
                pairs = minus_maxima_cols[:, job % 2, :, GR:GR + 2 * HG].rearrange("p t (h s) -> p t h s", s=2)
                dve.tensor_scalar(pairs[:, :, :, 0].bitcast(F32R), maxima[:, job % 2], -1.0, None, ALU.mult)\
                    .then_inc(maxima_high_done, 1)
                dve.wait_ge(maxima_high_done, job + 1)
                dve.scalar_tensor_tensor(out=pairs[:, :, :, 1].bitcast(F32R), in0=maxima[:, job % 2], scalar=-1.0,
                                         in1=pairs[:, :, :, 0], op0=ALU.mult, op1=ALU.subtract)\
                    .then_inc(maxima_low_done, 1)

            def divide(n, t):
                tile = filled(("back", n, t))[:].rearrange("p (h c) -> p h c", c=VC)
                dve.reciprocal(recip[:, t, :], tile[:, :, HD]).then_inc(recip_done, 1)
                dve.wait_ge(recip_done, n * TT + t + 1)
                dve.tensor_tensor(att[:, t, :].rearrange("p (h e) -> p h e", e=HD), tile[:, :, 0:HD],
                                  recip[:, t, :].rearrange("p (h o) -> p h o", o=1)
                                  .to_broadcast([P, H, HD]), ALU.mult).then_inc(dve_bank_read, 1)

            def first_residual(b):
                dve.wait_ge(dve_bank_read, DVE_USE[("back", SEQ.index((0, b)), 1)] + 1)
                dve.tensor_tensor(x1[b][:], xb[b][:], att[:], ALU.add).then_inc(x1_done, 1)
                dve.wait_ge(x1_done, b + 1)
                norm_stats(1, x1[b], b)

            def source(b):
                if b:
                    dve.wait_ge(src_bo_done, b)
                normalise(1, src, x1[b], b)

            def add_bias(b, t):
                if b == 0:
                    dve.wait_ge(weights_in, WEIGHTS_IN)
                else:
                    n = SEQ.index((1, b - 1))
                    dve.wait_ge(values_done, n + 1)
                    dve.wait_ge(queries_low_done, n + 1)
                tile = filled(("project", b, t))
                dve.tensor_tensor(qkv[:, t, :], tile[:, 0:3 * D], bqkv[:], ALU.add).then_inc(dve_bank_read, 1)

            def second_residual(b, t):
                dve.wait_ge(src_bo_done, b + 1)
                tile = filled(("out_project", b, t))
                dve.tensor_tensor(res[:, t, :], tile[:, 0:D], src_bo[b][:, t, :], ALU.add).then_inc(dve_bank_read, 1)

            def router(b):
                dve.wait_ge(h_done, (b + 1) * TT)
                done = b * ROUTER_STEPS
                for t in range(TT):
                    if done + t:
                        dve.wait_ge(route, done + t)
                    dve.scalar_tensor_tensor(out=junk[:], in0=h[:, t, :], scalar=1.0, in1=rw_b[:], op0=ALU.mult,
                                             op1=ALU.mult, accum_out=key[:, t:t + 1]).then_inc(route, 1)
                dve.wait_ge(route, done + 2)
                dve.tensor_scalar(key_b[:], key[:], rb_b[:, 0:1], None, ALU.add).then_inc(route, 1)
                dve.tensor_scalar(key_i[:], key[:], rb_b[:, 0:1], None, ALU.add).then_inc(route, 1)
                dve.wait_ge(route, done + 4)
                dve.tensor_tensor(key_gt[:], key_i[:], key_b[:], ALU.is_gt).then_inc(route, 1)
                dve.wait_ge(route, done + 5)
                dve.tensor_tensor(key_fi[:], key_i[:], key_gt[:], ALU.subtract).then_inc(route, 1)
                dve.wait_ge(route, done + 6)
                dve.tensor_scalar(expert[:], key_fi[:], NE - 1, None, ALU.bitwise_and).then_inc(route, 1)
                dve.wait_ge(route, done + 7)
                for e in range(NE):
                    dve.tensor_scalar(chosen[:, b % 2, e, :], expert[:], float(e), None, ALU.is_equal)\
                        .then_inc(route, 1)

            def add_expert(b, e):
                dve.wait_ge(down_done, b * 8 + 2 * (e + 1))
                if e == 0:
                    dve.wait_ge(route, (b + 1) * ROUTER_STEPS)
                    if b:
                        dve.wait_ge(gain_done[3], b * TT)
                else:
                    dve.wait_ge(acc_done, b * 8 + 2 * e)
                base = h if e == 0 else acc
                for t in range(TT):
                    dve.scalar_tensor_tensor(out=acc[:, t, :], in0=expert_bank(b, e)[:, t * D:(t + 1) * D],
                                             scalar=chosen[:, b % 2, e, t:t + 1], in1=base[:, t, :],
                                             op0=ALU.mult, op1=ALU.add).then_inc(acc_done, 1)

            def split_b2(part):
                if part == 0:
                    dve.wait_ge(expert_weights_in, EXPERT_WEIGHTS_IN)
                    dve.wait_ge(consts, 6)
                    dve.tensor_copy(b2_high[:], b2_twice[:]).then_inc(b2_step, 1)
                else:
                    dve.wait_ge(b2_step, 1)
                    dve.scalar_tensor_tensor(out=b2_rows[:].rearrange("r e d -> r (e d)"),
                                             in0=b2_high[:].bitcast(F32), scalar=b2_second[:, 0:1],
                                             in1=b2_twice[:], op0=ALU.mult, op1=ALU.add).then_inc(b2_step, 1)

            def h_low(b):
                dve.wait_ge(act_bank_read, ACT_USE[("h_t", b)] + 1)
                dve.tensor_tensor(h_low_t[b % 2][:], h_t[:], h_high_t[b % 2][:].bitcast(F32), ALU.subtract)\
                    .then_inc(h_low_done, 1)

            for s in range(LAST_STEP):
                for slot in range(4):
                    if s < JOBS:
                        maximum(s, slot)
                        if slot == 3:
                            minus_maxima(s)
                    if (s, slot) == (1, 0):
                        clear_values(2)
                    for n, t in due("back", s, slot):
                        divide(n, t)
                        if t == TT - 1 and SEQ[n][0] == 0:
                            first_residual(SEQ[n][1])
                    for b, t in due("project", s, slot):
                        add_bias(b, t)
                    for b, t in due("out_project", s, slot):
                        second_residual(b, t)
                        if t == TT - 1:
                            dve.wait_ge(dve_bank_read, DVE_USE[("out_project", b, t)] + 1)
                            norm_stats(2, res, b)
                            gained(2, res_g, res, g1_b)
                    for b, in due("source", s, slot):
                        source(b)
                    for b, in due("norm1_stats", s, slot):
                        norm1_stats(b)
                    for b, in due("norm1", s, slot):
                        norm1(b)
                    for b, e in due("expert_sum", s, slot):
                        add_expert(b, e)
                        if e == NE - 1:
                            dve.wait_ge(acc_done, b * 8 + 8)
                            norm_stats(3, acc, b)
                            gained(3, acc_g, acc, g2_b)
                            dve.wait_ge(x1_b2_done, b + 1)
                            scaled(3, x1[b], acc_g, [x1_b2[b][:, t, :] for t in range(TT)], b, out_done)
                    for b, in due("h", s, slot):
                        if b:
                            dve.wait_ge(acc_done, (b - 1) * 8 + 2)
                        scaled(2, h, res_g, [be1_b[:]] * TT, b, h_done)
                    for b, in due("h_t", s, slot):
                        h_low(b)
                    for b, in due("router", s, slot):
                        router(b)
                    for part, in due("b2", s, slot):
                        split_b2(part)

        @block.scalar
        def _(act):
            for b in range(2):
                act.dma_start(xb[b][:], xr[b]).then_inc(x_in[b], 16)

            def high_part(dst, v, slots, done):
                stack = dst[:].rearrange("p t (h s e) -> p t h s e", s=TERMS, e=HD)
                a, z = slots
                for t in range(TT):
                    ins = act.copy(stack[:, t, :, a:z + 1:z - a, :],
                                   by_head(v)[:, t].rearrange("p h (o e) -> p h o e", o=1)
                                   .to_broadcast([P, H, 2, HD]))
                ins.then_inc(done, 1)

            def keys_high(n):
                a, b = SEQ[n]
                if a == 0:
                    act.wait_ge(c_in[b], 16)
                else:
                    act.wait_ge(dve_bank_read, DVE_USE[("project", b, 1)] + 1)
                high_part(k_tok[n % 2], operands(n)[0], (0, 2), keys_high_done)

            def queries_high(n):
                a, b = SEQ[n]
                if a == 0:
                    act.wait_ge(norm_done[0], (b + 1) * TT)
                high_part(q_tok[n % 2], operands(n)[1], (0, 1), queries_high_done)

            def place_values(n):
                if n < 3:
                    act.wait_ge(values_clear, 2 * n + 1)
                else:
                    act.wait_ge(weighed, G * (n - 2))
                act.copy(values[n % 3][:, :, :, 0:HD], by_head(operands(n)[2])).then_inc(values_done, 1)

            def filled(use):
                act.wait_ge(act_bank_full, ACT_USE[use] + 1)
                return act_banks[ACT_USE[use] % ACT_BANKS]

            def max_rows(k, g):
                act.wait_ge(consts, 6)
                act.copy(keys_bd[k][GR:P, g, :, :],
                         head_rows[GR:P, :].rearrange("p (h o) -> p h o", o=1).to_broadcast([P - GR, HG, S]))\
                    .then_inc(max_rows_done, 1)

            def stacks(n, k):
                tile = filled(("stacks", n, k))
                dst = k_rows[n % 3][:, 2 * k:2 * k + 2, :] if k < 2 else \
                    q_rows[n % 3][0:GR, 2 * (k - 2):2 * (k - 2) + 2, :]
                act.copy(dst, tile[0:GR, :].rearrange("p (g s) -> p g s", s=S)).then_inc(act_bank_read, 1)

            def small(dst, use, rows=slice(0, P), cols=S):
                act.copy(dst, filled(use)[rows, 0:cols]).then_inc(act_bank_read, 1)

            def exps(job, j):
                if j == 0 and job >= 2:
                    act.wait_ge(weighed, job - 1)
                tile = filled(("scores", job, j))
                act.activation(probs[:, job % 2, j // 2, 2 * (j % 2):2 * (j % 2) + 2, :],
                               tile[:].rearrange("p (h q) -> p h q", q=S), ACT.Exp,
                               scale=SCALE2 if SEQ[job // G][0] else 1.0).then_inc(act_bank_read, 1)

            def evacuate_heads(job):
                k = job % G // 2
                act.wait_ge(weighed, job + 1)
                act.copy(heads_t[:, 2 * k:2 * k + 2, :], HEADS[:].rearrange("p (g s) -> p g s", s=S))\
                    .then_inc(heads_read, 1)

            def relu(b, u):
                if u >= 2:
                    act.wait_ge(down_done, b * 8 + (u - 1))
                tile = filled(("up", b, u))
                for c in range(2):
                    ins = act.activation(hid[:, u % 2, c, :], tile[:, c * S:(c + 1) * S], ACT.Relu,
                                         bias=b1_cols[:, 2 * u + c:2 * u + c + 1])
                ins.then_inc(act_bank_read, 1)

            keys_high(0)
            keys_high(1)
            for g in range(G // 2, G):
                max_rows(0, g)
            queries_high(0)
            for s in range(-1, LAST_STEP):
                if s == 0:
                    place_values(0)
                    queries_high(1)
                    place_values(1)
                if s - 4 >= 0 and (s - 4) % 2 == 1 and s - 4 < JOBS:
                    evacuate_heads(s - 4)
                for slot in range(4):
                    for n, k in due("stacks", s, slot):
                        stacks(n, k)
                    for b, in due("src_t", s, slot):
                        small(src_t[:], ("src_t", b))
                    for b, in due("att_t", s, slot):
                        small(att_t[:], ("att_t", b))
                    for b, in due("h_t", s, slot):
                        act.copy(h_high_t[b % 2][:], filled(("h_t", b))[:, 0:S])
                        if b:
                            act.wait_ge(h_low_done, b)
                        small(h_t[:], ("h_t", b))
                    if due("b1", s, slot):
                        small(b1_cols[:], ("b1",), cols=NE * FC)
                    if 0 <= s - 2 < JOBS:
                        exps(s - 2, slot)
                    if slot == TURN_SLOT and 0 <= s - 1 < JOBS:
                        n, g = divmod(s - 1, G)
                        small(q_rows[n % 3][GR:P, g, :], ("maxima", s - 1), rows=slice(GR, P))
                    for b, q in due("experts", s, slot):
                        if q < 2 * NE:
                            relu(b, q)
                    for n, in due("keys_high", s, slot):
                        keys_high(n)
                    for n, in due("queries_high", s, slot):
                        queries_high(n)
                    for n, in due("place_values", s, slot):
                        place_values(n)
                    for k, g in due("max_rows", s, slot):
                        max_rows(k, g)
                    for e, in due("w1_high", s, slot):
                        act.wait_ge(expert_weights_in, EXPERT_WEIGHTS_IN)
                        act.copy(w1_high[:, e, :], w1[:, e, :]).then_inc(w1_high_done, 1)

        @block.tensor
        def _(pe):
            def act_bank(use):
                n = ACT_USE[use]
                if n >= ACT_BANKS:
                    pe.wait_ge(act_bank_read, n - ACT_BANKS + 1)
                return act_banks[n % ACT_BANKS]

            def dve_bank(use):
                place, over = DVE_PLACE[use]
                if over:
                    pe.wait_ge(dve_bank_read, over)
                return dve_banks[place]

            def single(done, n):
                if n >= 1:
                    pe.wait_ge(done, n)

            def stacks(n, k):
                if k % 2 == 0:
                    pe.wait_ge(keys_low_done if k < 2 else queries_low_done, n + 1)
                tok = (k_tok if k < 2 else q_tok)[n % 2]
                tile = act_bank(("stacks", n, k))
                for g in range(2):
                    for t in range(TT):
                        c = (2 * (k % 2) + g) * GR
                        ins = pe.transpose(tile[0:GR, g * S + t * P:g * S + (t + 1) * P].bitcast(F32R),
                                           tok[:, t, c:c + GR], ident_r[:])
                ins.then_inc(act_bank_full, 1)

            def query_major(job, j):
                n, g = divmod(job, G)
                qt, pr = divmod(j, 2)
                if j == 0:
                    pe.wait_ge(act_bank_read, ACT_USE[("stacks", n, 2 + g // 2)] + 1)
                if qt == 0:
                    if job < 2:
                        pe.wait_ge(first_blocks_done, 2 * pr + 2)
                    else:
                        pe.wait_ge(blocks_done, 8 * n - 4 + 4 * (g // 2) + 2 * pr + 2)
                tile = dve_bank(("scores", job, j))
                ins = pe.matmul(tile[:], q_rows[n % 3][0:GR, g, qt * P:(qt + 1) * P],
                                keys_bd[n % 3][0:GR, g, 2 * pr:2 * pr + 2, :], start=True, stop=True)
                if SEQ[n][0] == 0:
                    kt = 1 - qt
                    tri = tile[:].rearrange("p (h k) -> p h k", k=S)[:, :, kt * P:(kt + 1) * P]
                    ins = pe.matmul(tri, ident_b[:], (mask_above, mask_below)[qt][:],
                                    start=False, stop=True, skip_group_check=True)
                ins.then_inc(dve_bank_full, 1)

            def turn_maxima(job):
                pe.wait_ge(maxima_low_done, job + 1)
                tile = act_bank(("maxima", job))
                for qt in range(TT):
                    ins = pe.transpose(tile[:, qt * P:(qt + 1) * P].bitcast(F32R),
                                       minus_maxima_cols[:, job % 2, qt, :].bitcast(F32R), ident_r[:])
                ins.then_inc(act_bank_full, 1)

            def key_major(job, j):
                n, g = divmod(job, G)
                kb, pr = divmod(j, 2)
                if j == 0:
                    pe.wait_ge(act_bank_read, ACT_USE[("maxima", job)] + 1)
                tile = act_bank(("scores", job, j))
                for i in range(2):
                    ins = pe.matmul(tile[:, i * S:(i + 1) * S],
                                    keys_bd[n % 3][:, g, 2 * pr + i, kb * P:(kb + 1) * P],
                                    q_rows[n % 3][:, g, :], start=True, stop=True)
                ins.then_inc(act_bank_full, 1)

            def weigh(job, kb):
                n, g = divmod(job, G)
                if SEQ[n][0] == 0:
                    pe.wait_ge(window_done, 2 * (FIRST_JOBS.index(job)) + kb + 1)
                pe.wait_ge(act_bank_read, ACT_USE[("scores", job, 2 * kb + 1)] + 1)
                if g == 0 and kb == 0:
                    pe.wait_ge(values_done, n + 1)
                    if n < 3:
                        pe.wait_ge(values_clear, 2 * n + 2)
                if g % 2 == 0 and kb == 0:
                    single(heads_read, job // 2)
                for hh in range(HG):
                    ins = pe.matmul(HEADS[VC * hh:VC * (hh + 1), (g % 2) * S:(g % 2 + 1) * S],
                                    values[n % 3][:, kb, HG * g + hh, :], probs[:, job % 2, kb, hh, :],
                                    start=(kb == 0), stop=(kb == TT - 1))
                if kb == TT - 1:
                    ins.then_inc(weighed, 1)

            def back(n, t):
                pe.wait_ge(heads_read, 2 * n + 2)
                tile = dve_bank(("back", n, t))
                for g in range(G):
                    ins = pe.transpose(tile[:, g * P:(g + 1) * P], heads_t[:, g, t * P:(t + 1) * P],
                                       ident[:])
                ins.then_inc(dve_bank_full, 1)

            def turn_small(v, use):
                tile = act_bank(use)
                for t in range(TT):
                    ins = pe.transpose(tile[:, t * P:(t + 1) * P], v[:, t, :], ident[:])
                ins.then_inc(act_bank_full, 1)

            def project(lhs, rhs, width, t, of, use):
                pe.wait_ge(act_bank_read, ACT_USE[of] + 1)
                pe.matmul(dve_bank(use)[:, 0:width], lhs[:, t * P:(t + 1) * P], rhs[:], start=True, stop=True)\
                    .then_inc(dve_bank_full, 1)

            def up(b, u):
                if u == 0:
                    pe.wait_ge(h_low_done, b + 1)
                tile = act_bank(("up", b, u))
                e = u // 2
                if b == 0:
                    pe.wait_ge(w1_low_done, e + 1)
                for c in range(2):
                    f = (2 * (u % 2) + c) * P
                    out_c = tile[:, c * S:(c + 1) * S]
                    pe.matmul(out_c, w1_high[:, e, f:f + P], h_high_t[b % 2][:], start=True, stop=False)
                    pe.matmul(out_c, w1_high[:, e, f:f + P], h_low_t[b % 2][:], start=False, stop=False)
                    ins = pe.matmul(out_c, w1_low[:, e, f:f + P], h_high_t[b % 2][:],
                                    start=False, stop=True)
                ins.then_inc(act_bank_full, 1)

            def down(b, u):
                e = u // 2
                to = expert_bank(b, e)
                if u % 2 == 0:
                    if (b, e) == (2, 1):
                        pe.wait_ge(heads_read, JOBS // 2)
                    elif b < 2 or (b, e) == (2, 0):
                        single(acc_done, b * 8 + 2 * e)
                        if (b, e) == (0, 0):
                            pe.wait_ge(dve_bank_read, DVE_USE[("scores", FIRST_EXPERT, 0)])
                    else:
                        pe.wait_ge(acc_done, b * 8 + 2 * e - 2)
                    pe.matmul(to[:, 0:TT * D], ones_r[:],
                              b2_rows[:, e, :].rearrange("r (o d) -> r o d", o=1).to_broadcast([2, TT, D]),
                              start=True, stop=False, skip_group_check=True)
                pe.wait_ge(act_bank_read, ACT_USE[("up", b, u)] + 1)
                for c in range(2):
                    for t in range(TT):
                        ins = pe.matmul(to[:, t * D:(t + 1) * D], hid[:, u % 2, c, t * P:(t + 1) * P],
                                        w2[:, e, 2 * (u % 2) + c, :], start=False,
                                        stop=(u % 2 == 1 and c == 1), skip_group_check=True)
                ins.then_inc(down_done, 1)

            pe.wait_ge(dve_idents, 1)
            for s in range(-1, LAST_STEP):
                if s == 0:
                    pe.wait_ge(consts, 6)
                    pe.wait_ge(dve_idents, 3)
                if s >= 2 and s % G == 2 and s // G < 3:
                    if s < G:
                        pe.wait_ge(dve_consts, DVE_CONSTS)
                    pe.wait_ge(max_rows_done, G // 2 + G * (s // G))
                for slot in range(4):
                    if 0 <= s < JOBS:
                        query_major(s, slot)
                    for n, t in due("back", s, slot):
                        back(n, t)
                    for b, t in due("project", s, slot):
                        if b == 0:
                            pe.wait_ge(weights_in, WEIGHTS_IN)
                        project(src_t, wqkv, 3 * D, t, ("src_t", b), ("project", b, t))
                    for b, t in due("out_project", s, slot):
                        project(att_t, wo, D, t, ("att_t", b), ("out_project", b, t))
                    for n, k in due("stacks", s, slot):
                        stacks(n, k)
                    for b, in due("src_t", s, slot):
                        pe.wait_ge(norm_done[1], (b + 1) * TT)
                        turn_small(src, ("src_t", b))
                    for b, in due("att_t", s, slot):
                        pe.wait_ge(dve_bank_read, DVE_USE[("back", SEQ.index((1, b)), 1)] + 1)
                        turn_small(att, ("att_t", b))
                    for b, in due("h_t", s, slot):
                        pe.wait_ge(h_done, (b + 1) * TT)
                        turn_small(h, ("h_t", b))
                    if due("b1", s, slot):
                        pe.wait_ge(expert_weights_in, EXPERT_WEIGHTS_IN)
                        pe.transpose(act_bank(("b1",))[:, 0:NE * FC], b1_rows[:],
                                     ident[0:NE * FC, 0:NE * FC]).then_inc(act_bank_full, 1)
                    if 0 <= s - 2 < JOBS:
                        key_major(s - 2, slot)
                    if slot == TURN_SLOT and 0 <= s - 1 < JOBS:
                        turn_maxima(s - 1)
                    if slot % 2 == 1 and 0 <= s - 3 < JOBS:
                        weigh(s - 3, slot // 2)
                    for b, q in due("experts", s, slot):
                        if q < 2 * NE:
                            up(b, q)
                        if q > 0:
                            if q == 1 and b == 0:
                                pe.wait_ge(b2_step, 2)
                            down(b, q - 1)


_INS = ["x", "ctx_1024"] + ["L0_ffn_" + n for n in (
    "Wq", "bq", "Wk", "bk", "Wv", "bv", "Wo", "bo", "router_w", "router_b", "W1", "b1", "W2", "b2",
    "ln1_g", "ln1_b", "ln2_g", "ln2_b")]


def kernel(**inputs):
    import concourse.bacc as bacc
    from concourse.bass_utils import run_bass_kernel_spmd

    nc = bacc.Bacc("TRN2", target_bir_lowering=False, num_devices=1)
    arrays, args = {}, []
    for name in _INS:
        a = np.ascontiguousarray(inputs[name])
        arrays[f"in_{name}"] = a
        args.append(nc.dram_tensor(f"in_{name}", a.shape, mybir.dt.from_np(a.dtype), kind="ExternalInput").ap())
    args.append(nc.dram_tensor("out_0", (B, S, D), F32, kind="ExternalOutput").ap())
    build(nc, *args)
    r = run_bass_kernel_spmd(nc, [arrays], core_ids=[0])
    return r.results[0]["out_0"]
```
